# Optimizing a Trainium2 kernel written in Bass

```python
import numpy as np
import jax
import jax.numpy as jnp

def _softmax(x, axis=-1):
    return jax.nn.softmax(x, axis=axis)

def _gelu(x):
    return jax.nn.gelu(x, approximate=True)

def _silu(x):
    return jax.nn.silu(x)

def _sigmoid(x):
    return jax.nn.sigmoid(x)

def _layernorm(x, axis=-1, eps=1e-05):
    m = jnp.mean(x, axis=axis, keepdims=True)
    v = jnp.var(x, axis=axis, keepdims=True)
    return (x - m) / jnp.sqrt(v + eps)

def _scatter_add(tgt, idx, src, axis=0):
    return tgt.at[idx].add(src)

def _segment_sum(src, seg, n):
    return jax.ops.segment_sum(src, seg, n)
kernel_name = 'mk_xattn_ffn_d1_seqx_r4_8e1ab7'

def setup_inputs(seed: int=0):
    np.random.seed(seed)
    _w = jnp.asarray

    def _rec_inputs():
        import jax
        import jax.numpy as jnp
        _rk = jax.random.key(seed)
        x = 4.136e-05 + 0.9999 * jax.random.normal(jax.random.fold_in(_rk, 1), (64, 256, 256), jnp.float32)
        _lenS = 256 - jax.random.randint(jax.random.fold_in(_rk, 7), (64,), 0, max(1, 256 // 4) + 1, jnp.int32)
        _lenS2 = 120 - jax.random.randint(jax.random.fold_in(_rk, 8), (64,), 0, max(1, 120 // 4) + 1, jnp.int32)
        _ctx_1024P = jax.random.normal(jax.random.fold_in(_rk, 11), (64, 16, 256), jnp.float32)
        _ctx_1024c = jax.random.dirichlet(jax.random.fold_in(_rk, 511), 0.3 * jnp.ones((16,), jnp.float32), (64, 120))
        _ctx_1024t = jnp.einsum('bsk,bkd->bsd', _ctx_1024c, _ctx_1024P)
        _ctx_1024t = _ctx_1024t * jax.lax.rsqrt(jnp.mean(jnp.square(_ctx_1024t)) + 1e-12) * 0.953939
        ctx_1024 = 7.22013e-05 + 1.00017 * (_ctx_1024t + 0.3 * jax.random.normal(jax.random.fold_in(_rk, 611), (64, 120, 256), jnp.float32))
        return (x, ctx_1024)
    x, ctx_1024 = _rec_inputs()

    def _L0_xattn_setup():
        import jax, jax.numpy as jnp
        import numpy as np
        D_MODEL = 256
        N_HEADS = 16
        D_HEAD = D_MODEL // N_HEADS
        LN_EPS = 1e-05

        def layer_norm(x, gamma, beta):
            mu = jnp.mean(x, axis=-1, keepdims=True)
            var = jnp.mean(jnp.square(x - mu), axis=-1, keepdims=True)
            return (x - mu) * jax.lax.rsqrt(var + LN_EPS) * gamma + beta
        key = jax.random.key(seed)
        ks = jax.random.split(key, 8)
        B, T = (4, 512)
        s = 1.0 / np.sqrt(D_MODEL)
        return {'encoder_seq': jax.random.normal(ks[0], (B, T, D_MODEL), jnp.float32), 'decoder_seq': jax.random.normal(ks[1], (B, T, D_MODEL), jnp.float32), 'Wq': jax.random.normal(ks[2], (D_MODEL, D_MODEL), jnp.float32) * s, 'bq': jnp.zeros((D_MODEL,), jnp.float32), 'Wk': jax.random.normal(ks[3], (D_MODEL, D_MODEL), jnp.float32) * s, 'bk': jnp.zeros((D_MODEL,), jnp.float32), 'Wv': jax.random.normal(ks[4], (D_MODEL, D_MODEL), jnp.float32) * s, 'bv': jnp.zeros((D_MODEL,), jnp.float32), 'ln_gamma': jnp.ones((D_MODEL,), jnp.float32), 'ln_beta': jnp.zeros((D_MODEL,), jnp.float32)}
    _L0_xattn_all = _L0_xattn_setup()
    _L0_xattn_in = {k: v for k, v in _L0_xattn_all.items() if k in ('Wq', 'bq', 'Wk', 'bk', 'Wv', 'bv', 'ln_gamma', 'ln_beta')}
    del _L0_xattn_all

    def _L0_ffn_setup():
        import jax, jax.numpy as jnp
        import numpy as np
        B, S, H, E = (2, 512, 256, 16)
        key = jax.random.key(seed)
        k0, k1, k2, k3 = jax.random.split(key, 4)
        tokens = jax.random.normal(k0, (B, S, H), dtype=jnp.float32)
        gate_w = jax.random.normal(k1, (E, H), dtype=jnp.float32) * H ** (-0.5)
        expert_w = jax.random.normal(k2, (E, H, H), dtype=jnp.float32) * H ** (-0.5)
        expert_b = jax.random.normal(k3, (E, H), dtype=jnp.float32) * 0.01
        return {'tokens': tokens, 'gate_w': gate_w, 'expert_w': expert_w, 'expert_b': expert_b}
    _L0_ffn_all = _L0_ffn_setup()
    _L0_ffn_in = {k: v for k, v in _L0_ffn_all.items() if k in ('gate_w', 'expert_w', 'expert_b')}
    del _L0_ffn_all
    return {'x': x, 'ctx_1024': ctx_1024, 'L0_xattn_Wq': _L0_xattn_in['Wq'], 'L0_xattn_bq': _L0_xattn_in['bq'], 'L0_xattn_Wk': _L0_xattn_in['Wk'], 'L0_xattn_bk': _L0_xattn_in['bk'], 'L0_xattn_Wv': _L0_xattn_in['Wv'], 'L0_xattn_bv': _L0_xattn_in['bv'], 'L0_xattn_ln_gamma': _L0_xattn_in['ln_gamma'], 'L0_xattn_ln_beta': _L0_xattn_in['ln_beta'], 'L0_ffn_gate_w': _L0_ffn_in['gate_w'], 'L0_ffn_expert_w': _L0_ffn_in['expert_w'], 'L0_ffn_expert_b': _L0_ffn_in['expert_b']}

def reference(x, ctx_1024, L0_xattn_Wq, L0_xattn_bq, L0_xattn_Wk, L0_xattn_bk, L0_xattn_Wv, L0_xattn_bv, L0_xattn_ln_gamma, L0_xattn_ln_beta, L0_ffn_gate_w, L0_ffn_expert_w, L0_ffn_expert_b):
    import jax
    import jax.numpy as jnp

    def _L0_xattn_ref(encoder_seq, decoder_seq, Wq, bq, Wk, bk, Wv, bv, ln_gamma, ln_beta):
        import jax, jax.numpy as jnp
        import numpy as np
        D_MODEL = 256
        N_HEADS = 16
        D_HEAD = D_MODEL // N_HEADS
        LN_EPS = 1e-05

        def layer_norm(x, gamma, beta):
            mu = jnp.mean(x, axis=-1, keepdims=True)
            var = jnp.mean(jnp.square(x - mu), axis=-1, keepdims=True)
            return (x - mu) * jax.lax.rsqrt(var + LN_EPS) * gamma + beta
        B, T_dec, _ = decoder_seq.shape
        T_enc = encoder_seq.shape[1]
        q = (decoder_seq @ Wq.T + bq).reshape(B, T_dec, N_HEADS, D_HEAD)
        k = (encoder_seq @ Wk.T + bk).reshape(B, T_enc, N_HEADS, D_HEAD)
        v = (encoder_seq @ Wv.T + bv).reshape(B, T_enc, N_HEADS, D_HEAD)
        scale = 1.0 / np.sqrt(D_HEAD)
        kv = jnp.einsum('bthd,bthe->bhde', k, v)
        att = jnp.einsum('bqhd,bhde->bqhe', q, kv) * scale
        att = att.reshape(B, T_dec, D_MODEL)
        return layer_norm(att + decoder_seq, ln_gamma, ln_beta)

    def _L0_ffn_ref(tokens, gate_w, expert_w, expert_b):
        import jax, jax.numpy as jnp
        import numpy as np
        B, S, H, E = (2, 512, 256, 16)
        b, s, h = tokens.shape
        logits = jnp.einsum('bsh,eh->bse', tokens, gate_w)
        weights = jax.nn.softmax(logits, axis=-1)
        top2_w, top2_idx = jax.lax.top_k(weights, 2)
        flat = tokens.reshape(b * s, h)
        flat_w = top2_w.reshape(b * s, 2)
        flat_idx = top2_idx.reshape(b * s, 2)
        y = jax.nn.relu(jnp.einsum('nh,edh->ned', flat, expert_w) + expert_b[None, :, :])
        sel = jnp.take_along_axis(y, flat_idx[:, :, None], axis=1)
        out = jnp.sum(sel * flat_w[:, :, None], axis=1)
        return out.reshape(b, s, h)
    x = x + _L0_xattn_ref(ctx_1024, _layernorm(x, axis=-1), L0_xattn_Wq, L0_xattn_bq, L0_xattn_Wk, L0_xattn_bk, L0_xattn_Wv, L0_xattn_bv, L0_xattn_ln_gamma, L0_xattn_ln_beta)
    x = x + _L0_ffn_ref(_layernorm(x, axis=-1), L0_ffn_gate_w, L0_ffn_expert_w, L0_ffn_expert_b)
    return x

_drawn_inputs = setup_inputs


def setup_inputs(seed=0):
    import zlib

    import numpy as np

    out = dict(_drawn_inputs(seed))
    spreads = {'L0_xattn_bq': (0.0, 0.1),
     'L0_xattn_bk': (0.0, 0.1),
     'L0_xattn_bv': (0.0, 0.1),
     'L0_xattn_ln_gamma': (1.0, 0.2),
     'L0_xattn_ln_beta': (0.0, 0.1)}
    factors = {'L0_ffn_expert_b': 38.448}
    for name, (base, spread) in spreads.items():
        noise = np.random.default_rng([zlib.crc32(name.encode()), seed]).standard_normal(out[name].shape)
        drawn = base * np.exp(spread * noise) if base else spread * noise
        out[name] = jnp.asarray(drawn.astype(out[name].dtype))
    for name, factor in factors.items():
        out[name] = (out[name] * factor).astype(out[name].dtype)
    return out
```

```python
from contextlib import ExitStack

import concourse.bass as bass
from concourse import mybir

F32 = mybir.dt.float32
BF16 = mybir.dt.bfloat16
I32 = mybir.dt.int32
U32 = mybir.dt.uint32
ALU = mybir.AluOpType
ACT = mybir.ActivationFunctionType
AX_X = mybir.AxisListType.X

P = 128
NB, S, D = 64, 256, 256
SC = 120
NH = 16
E = 16
NT = S // P
KC = D // P
TOK = NB * S
SCALE = (D // NH) ** -0.5
EPS = 1e-5

ROW = D + 4
W_COL, ID_COL = D, D + 2
PAD = P
REGION = TOK + 2 * PAD
TILES = TOK // P + E
SPARE = E // 2 * REGION
ROWS = SPARE + E * P
PAD_ID = TOK
OUT_ROWS = TOK + 2 * E * P

U = 4
LEAD, LOOPS = 8, (NB - 4 - 8) // U
V = 8
LOG_EXP_SET = 6


class Batch:

    def __init__(self, i, c):
        self.i, self.c = i, c

    def __sub__(self, n):
        return Batch(self.i, self.c - n)

    def __add__(self, n):
        return Batch(self.i, self.c + n)

    def exists(self, low=0):
        return self.i is not None or low <= self.c < NB

    def times(self, k, plus=0):
        n = k * self.c + plus
        return n if self.i is None else self.i * (k * U) + n

    def uses(self, bufs, k):
        n = k * (self.c // bufs + 1)
        return n if self.i is None else self.i * (k * U // bufs) + n

    def buf(self, bufs):
        return self.c % bufs


def settle(eng, passed):
    eng.sem_inc(passed, 1)


def dense_steps(eng, step, low, high):
    for s in range(low, LEAD):
        step(Batch(None, s))
    with eng.Fori(0, LOOPS) as i:
        for j in range(U):
            step(Batch(i, LEAD + j))
    for s in range(LEAD + LOOPS * U, high):
        step(Batch(None, s))


def expert_steps(eng, step, k, peel_first=False, peel_last=False):
    first, last = int(peel_first), TILES // V - int(peel_last)
    if peel_first:
        for j in range(V):
            step(k, j, 0)
    with eng.Fori(first, last) as i:
        for j in range(V):
            step(k, j, i)
    if peel_last:
        for j in range(V):
            step(k, j, last)


def build(nc, x, ctx_t, wkv_t, wq_t, gate_t, we_t, bkv, be, bq, gamma, beta, out):
    bins = [nc.dram_tensor(f"bins{k}", [ROWS, ROW], F32, kind="Internal").ap() for k in range(2)]
    bkv_dram = nc.dram_tensor("bkv_dram", [3, 2 * D], BF16, kind="Internal").ap()
    be_dram = nc.dram_tensor("be_dram", [3, E * D], BF16, kind="Internal").ap()
    table_dram = nc.dram_tensor("table_dram", [1, 8 * P], I32, kind="Internal").ap()

    def parts_as_rows(dram):
        return dram.rearrange("n (p m) -> p n m", p=P)

    with ExitStack() as ctx:
        def sb(name, shape, dt=F32):
            return ctx.enter_context(nc.sbuf_tensor(name, shape, dt))

        def ps(name, shape, dt=F32):
            return ctx.enter_context(nc.psum_tensor(name, shape, dt))

        def sem(name):
            return ctx.enter_context(nc.semaphore(name))

        ident = sb("ident", [P, P])
        ones_row = sb("ones_row", [1, P])
        ones_bf = sb("ones_bf", [P, P], BF16)
        before = sb("before", [P, P], BF16)
        not_before = sb("not_before", [P, P], BF16)
        head_mask = sb("head_mask", [P, KC, P])
        iota_e = sb("iota_e", [P, E])
        tile_no = sb("tile_no", [P, 2])
        bin_base = sb("bin_base", [P, NT, 2, E])
        eps = sb("eps", [P, 1])
        wkv = sb("wkv", [P, KC, 2 * D])
        wq = sb("wq", [P, KC, D])
        wg = sb("wg", [P, KC, E])
        we = sb("we", [P, KC, E * D])
        bkv_rows = sb("bkv_rows", [P, 2 * D], BF16)
        be_rows = sb("be_rows", [P, E * D], BF16)
        bkv_in = sb("bkv_in", [P, 2 * D // P])
        be_in = sb("be_in", [P, E * D // P])
        bkv_rest = sb("bkv_rest", [P, 2, 2 * D // P])
        be_rest = sb("be_rest", [P, 2, E * D // P])
        bkv_part = sb("bkv_part", [P, 3, 2 * D // P], BF16)
        be_part = sb("be_part", [P, 3, E * D // P], BF16)
        bq_sb = sb("bq_sb", [P, KC])
        gamma_sb = sb("gamma_sb", [P, D])
        beta_sb = sb("beta_sb", [P, D])
        zeros = sb("zeros", [P, 1024])
        pad_rows = sb("pad_rows", [P, E, ROW])
        spare_rows = sb("spare_rows", [P, E, ROW])

        x_sb = sb("x_sb", [P, 4, NT, D])
        c_sb = sb("c_sb", [P, 4, KC, SC])
        h = sb("h", [P, 4, NT, D])
        h_t = sb("h_t", [P, KC, NT, P])
        kv = sb("kv", [SC, 2, D])
        q_t = sb("q_t", [P, KC, NT, P])
        kvm = sb("kvm", [P, KC, P])
        att = sb("att", [P, NT, D])
        scaled = sb("scaled", [P, NT, D])
        x_beta = sb("x_beta", [P, 2, NT, D])
        x1 = sb("x1", [P, 2, NT, D])
        rows = sb("rows", [P, 4, NT, ROW])
        h2_t = sb("h2_t", [P, KC, NT, P])
        st = sb("st", [P, 3, NT, 6])
        mv = sb("mv", [P, 3, 2, NT, 2])
        lnv = sb("lnv", [P, 3, NT])
        rstd = sb("rstd", [P, 3, 2, NT])
        nmr = sb("nmr", [P, 3, NT])
        top = sb("top", [P, NT, 8])
        top_i = sb("top_i", [P, NT, 8], U32)
        top_f = sb("top_f", [P, NT, 2])
        neg_max = sb("neg_max", [P, NT])
        gap = sb("gap", [P, NT])
        exps = sb("exps", [P, NT, E])
        sums = sb("sums", [P, NT])
        exp_gap = sb("exp_gap", [P, NT])
        onehot = sb("onehot", [P, 2, NT, 2, E], BF16)
        picked = sb("picked", [P, NT * 2, E])
        signed_pos = sb("signed_pos", [P, NT * 2])
        pos = sb("pos", [P, 2, NT, 2], I32)

        ends = sb("ends", [P, 2, E])
        counts = sb("counts", [P, 2, E])
        pad_at = sb("pad_at", [P, 2, E], I32)
        cnt_i = sb("cnt_i", [P, 2, E], I32)
        tiles_i = sb("tiles_i", [P, 2, E], I32)
        tiles_f = sb("tiles_f", [P, 2, E])
        scan = sb("scan", [P, 2, 2, E])
        shift = sb("shift", [P, 2, E + 1])
        delta = sb("delta", [P, 2, E])
        reached = sb("reached", [P, 2, 2, E])
        reached_d = sb("reached_d", [P, 2, 2, E])
        found = sb("found", [P, 2, 2, 2])
        table8 = sb("table8", [8, P], I32)
        table = sb("table", [1, 2, 2, 2 * P], I32)

        row_in = sb("row_in", [P, V, ROW])
        row_t = sb("row_t", [P, 2, KC, P])
        y = sb("y", [P, V, D])

        ps_ht = ps("ps_ht", [P, KC, NT, P])
        ps_kv = ps("ps_kv", [P, 2 * D])
        ps_q = [ps(f"ps_q{n}", [P, 512]) for n in range(KC)]
        ps_mg = ps("ps_mg", [P, 512])
        ps_att = ps("ps_att", [P, NT, D])
        ps_h2t = ps("ps_h2t", [P, KC, NT, P])
        ps_rank = ps("ps_rank", [P, 512])
        ktv = ps_mg[:, 0:D]
        logits = ps_mg[:, D:D + NT * E].rearrange("p (t e) -> p t e", e=E)
        rank = ps_rank[:, 0:NT * 2 * E].rearrange("p (t c e) -> p t c e", t=NT, e=E)
        ps_rt = [ps_ht, ps_h2t]
        ps_y = [ps_att[:, 0, :], ps_q[0][:, 0:D]]

        s_w = [sem(f"weights{n}_loaded") for n in range(5)]
        s_be_in = sem("expert_bias_loaded")
        s_const = sem("pool_constants_made")
        s_step = sem("pool_step_done")
        s_passed = [sem(f"passed_by_{n}") for n in ("dve", "pool")]
        s_zero = sem("zeros_made")
        s_split = sem("bias_split_step")
        s_kvb = sem("kv_bias_rows_placed")
        s_eb = sem("expert_bias_rows_placed")
        s_kvd = sem("kv_bias_parts_in_dram")
        s_ebd = sem("expert_bias_parts_in_dram")
        s_tabd = sem("table_in_dram")
        s_init = sem("dram_fill_written")
        s_rank0 = sem("rank_started")
        s_x = [sem(f"x_loaded{n}") for n in range(4)]
        s_c = [sem(f"context_loaded{n}") for n in range(4)]
        s_x1w = [sem(f"x1_written{n}") for n in range(2)]
        s_row = [sem(f"rows_scattered{n}") for n in range(4)]
        s_st = [sem(f"stats{n}_ready") for n in range(3)]
        s_mv = [sem(f"moments{n}_ready") for n in range(3)]
        s_ln = [sem(f"log_var{n}_ready") for n in range(3)]
        s_rstd = [sem(f"rstd{n}_ready") for n in range(3)]
        s_nmr = {0: sem("shift0_ready"), 2: sem("shift2_ready")}
        s_h = sem("h_ready")
        s_pht = sem("h_transposed")
        s_ht = sem("h_t_copied")
        s_pkv = sem("kv_projected")
        s_kv = sem("kv_copied")
        s_pq = sem("q_projected")
        s_q = sem("q_copied")
        s_pm = sem("ktv_multiplied")
        s_m = sem("ktv_masked")
        s_patt = sem("attention_multiplied")
        s_att = sem("attention_residual_ready")
        s_scaled = sem("scaled_ready")
        s_xb = sem("x_beta_ready")
        s_x1 = sem("x1_ready")
        s_h2 = sem("h2_ready")
        s_ph2t = sem("h2_transposed")
        s_h2t = sem("h2_t_copied")
        s_pg = sem("logits_ready")
        s_top = sem("top_values_ready")
        s_topi = sem("top_indices_ready")
        s_gap = sem("gap_ready")
        s_topf = sem("indices_as_floats")
        s_oh = sem("onehot_ready")
        s_exp = sem("exps_ready")
        s_w0 = sem("first_weight_ready")
        s_w1 = sem("second_weight_ready")
        s_id = sem("ids_advanced")
        s_prk = sem("ranks_ready")
        s_pick = sem("rank_picked")
        s_sum = sem("signed_position_ready")
        s_pos = sem("positions_ready")
        s_end = sem("rank_ends_ready")
        s_pad = sem("pad_positions_ready")
        s_padw = sem("pad_rows_written")
        s_tab = sem("table_step")
        s_found = sem("table_columns_ready")
        s_tt = sem("table_transposed")
        s_t8 = sem("table_copied")
        s_table = sem("table_placed")
        s_in = [sem(f"row_tile_loaded{n}") for n in range(V)]
        s_prt = sem("row_tile_transposed")
        s_rt = sem("row_tile_copied")
        s_py = sem("expert_multiplied")
        s_y = sem("expert_result_ready")
        s_add = [sem(f"result_added{n}") for n in range(V)]

        x_v = x.rearrange("(n p t) d -> n p t d", p=P, t=NT)
        out_v = out[0:TOK, :].rearrange("(n p t) d -> n p t d", p=P, t=NT)

        def batch_of(view, b):
            if b.i is None:
                return view[b.c]
            return view[bass.ds(b.times(1), 1)].rearrange("o p a d -> (o p) a d")

        block = ctx.enter_context(nc.Block())

        @block.sync
        def _(sp):
            def load(b):
                n = b.buf(4)
                if b.i is not None or b.c >= 4:
                    sp.wait_ge(s_xb, (b - 4).times(1, 1))
                    sp.wait_ge(s_h, (b - 4).times(1, 1))
                    sp.wait_ge(s_pkv, (b - 4).times(1, 1))
                sp.dma_start(x_sb[:, n], batch_of(x_v, b)).then_inc(s_x[n], 16)
                sp.dma_start(c_sb[:, n], batch_of(ctx_t, b)).then_inc(s_c[n], 16)

            load(Batch(None, 0))
            sp.dma_start(wkv[:], wkv_t.rearrange("(c p) n -> p c n", p=P)).then_inc(s_w[0], 16)
            sp.dma_start(bkv_in[:], bkv.rearrange("(p n) -> p n", p=P)).then_inc(s_w[1], 16)
            sp.dma_start(wq[:], wq_t.rearrange("(c p) n -> p c n", p=P)).then_inc(s_w[2], 16)
            sp.dma_start(bq_sb[:], bq).then_inc(s_w[2], 16)
            sp.dma_start(beta_sb[:], beta.partition_broadcast(P)).then_inc(s_w[3], 16)
            sp.dma_start(gamma_sb[:], gamma.partition_broadcast(P)).then_inc(s_w[3], 16)
            sp.dma_start(wg[:], gate_t.rearrange("(c p) n -> p c n", p=P)).then_inc(s_w[3], 16)
            load(Batch(None, 1))
            sp.wait_ge(s_zero, 3)
            sp.wait_ge(s_split, 5)
            sp.dma_start(parts_as_rows(bkv_dram), bkv_part[:]).then_inc(s_kvd, 16)
            sp.wait_ge(s_kvd, 16)
            sp.dma_start(bkv_rows[0:65:32, :], bkv_dram).then_inc(s_kvb, 16)
            load(Batch(None, 2))
            load(Batch(None, 3))
            sp.dma_start(be_in[:], be.rearrange("(p n) -> p n", p=P)).then_inc(s_be_in, 16)
            sp.dma_start(we[:], we_t.rearrange("(c p) n -> p c n", p=P)).then_inc(s_w[4], 16)
            sp.wait_ge(s_zero, 1)
            tail = out[TOK:OUT_ROWS, :].rearrange("(n p a) d -> n p (a d)", p=P, a=4)
            for n in range(OUT_ROWS // P // 4 - TOK // P // 4):
                sp.dma_start(tail[n], zeros[:]).then_inc(s_init, 16)
            sp.wait_ge(s_const, 1)
            for k in range(2):
                sp.dma_start(bins[k][SPARE:ROWS, :].rearrange("(j p) d -> p j d", p=P),
                             spare_rows[:]).then_inc(s_init, 16)

            def step(s):
                p = s - 1
                if p.exists():
                    sp.wait_ge(s_x1, p.times(1, 1))
                    sp.dma_start(batch_of(out_v, p), x1[:, p.buf(2)]).then_inc(s_x1w[p.buf(2)], 16)
                nxt = s + 4
                if nxt.exists():
                    load(nxt)
                if s.i is None and s.c == 2:
                    sp.wait_ge(s_split, 10)
                    sp.dma_start(parts_as_rows(be_dram), be_part[:]).then_inc(s_ebd, 16)
                    sp.wait_ge(s_ebd, 16)
                    sp.dma_start(be_rows[0:65:32, :], be_dram).then_inc(s_eb, 16)

            dense_steps(sp, step, 0, NB + 1)

            def fill(k):
                sp.wait_ge(s_pad, 1)
                for e in range(E):
                    at = sp.value_load(pad_at[0:1, k, e:e + 1], min_val=0, max_val=SPARE - P)
                    sp.dma_start(bins[k][bass.ds(at, P), :], pad_rows[:, e, :]).then_inc(s_padw, 16)

            fill(0)
            fill(1)
            sp.wait_ge(s_t8, 1)
            sp.dma_start(table_dram.rearrange("o (r t) -> (o r) t", r=8), table8[:]).then_inc(s_tabd, 16)
            sp.wait_ge(s_tabd, 16)
            sp.dma_start(table[:].rearrange("o q c t -> o (q c t)"), table_dram).then_inc(s_table, 16)
            for n in range(4):
                sp.wait_ge(s_row[n], 64 * (NB // 4))
            sp.wait_ge(s_padw, 2 * E * 16)
            sp.wait_ge(s_init, 16 * (OUT_ROWS // P // 4 - TOK // P // 4 + 2))
            sp.wait_ge(s_table, 16)

            def tile_load(k, j, i):
                at = sp.value_load(table[0:1, 0, k, bass.ds(i * V + j, 1)], min_val=0, max_val=ROWS - P)
                if not (isinstance(i, int) and k == 0):
                    sp.wait_ge(s_add[j], i * 16 + 16 * k * (TILES // V))
                sp.dma_start(row_in[:, j, :], bins[k][bass.ds(at, P), :]).then_inc(s_in[j], 16)

            for k in range(2):
                expert_steps(sp, tile_load, k, peel_first=(k == 0))
            for j in range(V):
                sp.wait_ge(s_add[j], 2 * 16 * (TILES // V))
            for n in range(2):
                sp.wait_ge(s_x1w[n], 16 * (NB // 2))

        @block.gpsimd
        def _(pool):
            steps = [0]

            def done(ins):
                steps[0] += 1
                ins.then_inc(s_step, 1)
                pool.wait_ge(s_step, steps[0])

            done(pool.memset(ident[:], 0.0))
            done(pool.affine_select(out=ident[:], in_=ident[:], compare_op=ALU.not_equal, fill=1.0, base=0,
                                    pattern=[[-1, P]], channel_multiplier=1))
            done(pool.memset(ones_bf[:], 1.0))
            done(pool.memset(ones_row[:], 1.0))
            done(pool.affine_select(out=before[:], in_=ones_bf[:], compare_op=ALU.is_gt, fill=0.0, base=0,
                                    pattern=[[1, P]], channel_multiplier=-1))
            done(pool.affine_select(out=not_before[:], in_=ones_bf[:], compare_op=ALU.is_ge, fill=0.0, base=0,
                                    pattern=[[-1, P]], channel_multiplier=1))
            G = D // NH
            mask = head_mask[:].rearrange("p c (g j) -> p c g j", j=G)
            done(pool.memset(head_mask[:], SCALE))
            done(pool.affine_select(out=mask, in_=mask, compare_op=ALU.is_ge, fill=0.0, base=0,
                                    pattern=[[0, KC], [-G, P // G], [0, G]], channel_multiplier=1))
            done(pool.affine_select(out=mask, in_=mask, compare_op=ALU.is_ge, fill=0.0, base=G - 1,
                                    pattern=[[0, KC], [G, P // G], [0, G]], channel_multiplier=-1))
            done(pool.iota(iota_e[:], [[1, E]], base=0, channel_multiplier=0,
                           allow_small_or_imprecise_dtypes=True))
            done(pool.iota(tile_no[:], [[P, 2]], base=0, channel_multiplier=1,
                           allow_small_or_imprecise_dtypes=True))
            base = bin_base[:].rearrange("p t c (r o) -> p (t c) r o", o=2)
            done(pool.iota(base[:, :, :, 0], [[0, NT * 2], [REGION, E // 2]], base=0, channel_multiplier=0,
                           allow_small_or_imprecise_dtypes=True))
            done(pool.iota(base[:, :, :, 1], [[0, NT * 2], [-REGION, E // 2]], base=1 - REGION,
                           channel_multiplier=0, allow_small_or_imprecise_dtypes=True))
            done(pool.memset(rows[:, :, :, :], 0.0))
            ids = rows[:].bitcast(I32)[:, :, :, ID_COL]
            done(pool.iota(ids, [[S, 4], [1, NT]], base=0, channel_multiplier=NT))
            done(pool.memset(pad_rows[:], 0.0))
            done(pool.iota(pad_rows[:].bitcast(I32)[:, :, ID_COL], [[P, E]], base=PAD_ID, channel_multiplier=1))
            done(pool.memset(spare_rows[:], 0.0))
            pool.iota(spare_rows[:].bitcast(I32)[:, :, ID_COL], [[P, E]], base=PAD_ID + E * P,
                      channel_multiplier=1).then_inc(s_const, 1)
            pool.wait_ge(s_w[3], 48)

            def step(s):
                if s.exists():
                    n = s.buf(2)
                    pool.wait_ge(s_x[s.buf(4)], s.uses(4, 16))
                    if s.i is not None or s.c >= 2:
                        pool.wait_ge(s_x1, (s - 2).times(1, 1))
                    pool.tensor_tensor(x_beta[:, n], x_sb[:, s.buf(4)],
                                       beta_sb[:].unsqueeze(1).to_broadcast([P, NT, D]),
                                       ALU.add).then_inc(s_xb, 1)
                f = s - 3
                if f.exists():
                    pool.wait_ge(s_w1, f.times(1, 1))
                    pool.wait_ge(s_id, f.times(1, 1))
                    pool.wait_ge(s_pos, f.times(1, 1))
                    settle(pool, s_passed[1])
                    for t in range(NT):
                        for k in range(2):
                            pool.indirect_dma_start(
                                out=bins[k], in_=rows[:, f.buf(4), t, :],
                                out_offset=bass.IndirectOffsetOnAxis(ap=pos[:, f.buf(2), t, k:k + 1], axis=0),
                                in_offset=None).then_inc(s_row[f.buf(4)], 16)

            dense_steps(pool, step, 0, NB + 3)
            for n in range(2):
                pool.wait_ge(s_x1w[n], 16 * (NB // 2))

            def add(k, j, i):
                pool.wait_ge(s_y, i * V + (k * TILES + j + 1))
                settle(pool, s_passed[1])
                pool.indirect_dma_start(
                    out=out, in_=y[:, j, :],
                    out_offset=bass.IndirectOffsetOnAxis(ap=row_in[:, j, ID_COL:ID_COL + 1].bitcast(I32), axis=0),
                    in_offset=None, compute_op=ALU.add).then_inc(s_add[j], 16)

            expert_steps(pool, add, 0)
            for j in range(V):
                pool.wait_ge(s_add[j], 16 * (TILES // V))
            expert_steps(pool, add, 1)

        @block.tensor
        def _(pe):
            pe.wait_ge(s_const, 1)
            pe.matmul(ps_rank[:, 0:NT * 2 * E], ones_row[:], bin_base[0:1].rearrange("o t c e -> o (t c e)"),
                      start=True, stop=False, skip_group_check=True).then_inc(s_rank0, 1)

            def project_kv(s):
                n = s.buf(4)
                pe.wait_ge(s_c[n], s.uses(4, 16))
                if s.i is not None or s.c >= 1:
                    pe.wait_ge(s_kv, (s - 1).times(1, 1))
                elif s.c == 0:
                    pe.wait_ge(s_w[0], 16)
                    pe.wait_ge(s_kvb, 16)
                    pe.wait_ge(s_zero, 3)
                for c in range(KC):
                    pe.matmul(ps_kv[0:SC, :], c_sb[:, n, c, :], wkv[:, c, :], start=(c == 0), stop=False)
                pe.matmul(ps_kv[0:SC, :], ones_bf[:, 0:SC], bkv_rows[:], start=False, stop=True).then_inc(s_pkv, 1)

            def attend(b):
                pe.wait_ge(s_q, b.times(2, 2))
                pe.wait_ge(s_m, b.times(1, 1))
                if b.i is not None or b.c >= 1:
                    pe.wait_ge(s_att, (b - 1).times(1, 1))
                for t in range(NT):
                    for c in range(KC):
                        mm = pe.matmul(ps_att[:, t, c * P:(c + 1) * P], q_t[:, c, t, :], kvm[:, c, :],
                                       start=True, stop=True)
                mm.then_inc(s_patt, 1)

            def transpose_h(b):
                pe.wait_ge(s_h, b.times(1, 1))
                if b.i is not None or b.c >= 1:
                    pe.wait_ge(s_ht, (b - 1).times(1, 1))
                for c in range(KC):
                    for t in range(NT):
                        mm = pe.transpose(ps_ht[:, c, t, :], h[:, b.buf(4), t, c * P:(c + 1) * P], ident[:])
                mm.then_inc(s_pht, 1)

            def multiply_ktv(b):
                pe.wait_ge(s_kv, b.times(1, 1))
                if b.i is not None or b.c >= 3:
                    pe.wait_ge(s_topi, (b - 3).times(1, 1))
                    pe.wait_ge(s_exp, (b - 3).times(1, 1))
                for c in range(KC):
                    mm = pe.matmul(ktv[:, c * P:(c + 1) * P], kv[:, 0, c * P:(c + 1) * P],
                                   kv[:, 1, c * P:(c + 1) * P], start=True, stop=True)
                mm.then_inc(s_pm, 1)

            def project_q(b, dc):
                if dc == 0:
                    if b.i is None and b.c == 0:
                        pe.wait_ge(s_w[2], 32)
                    pe.wait_ge(s_ht, b.times(1, 1))
                if b.i is not None or b.c >= 1:
                    pe.wait_ge(s_q, (b - 1).times(2, dc + 1))
                for c in range(KC):
                    mm = pe.matmul(ps_q[dc][:, 0:S], wq[:, c, dc * P:(dc + 1) * P], h_t[:, c, :, :],
                                   start=(c == 0), stop=(c == KC - 1))
                mm.then_inc(s_pq, 1)

            def transpose_h2(b):
                pe.wait_ge(s_h2, b.times(1, 1))
                if b.i is not None or b.c >= 1:
                    pe.wait_ge(s_h2t, (b - 1).times(1, 1))
                for c in range(KC):
                    for t in range(NT):
                        mm = pe.transpose(ps_h2t[:, c, t, :], rows[:, b.buf(4), t, c * P:(c + 1) * P], ident[:])
                mm.then_inc(s_ph2t, 1)

            def gate(b):
                pe.wait_ge(s_h2t, b.times(1, 1))
                pe.wait_ge(s_m, (b + 2).times(1, 1) if (b + 2).exists() else NB)
                if b.i is None and b.c >= NB - 2:
                    pe.wait_ge(s_topi, b.c)
                    pe.wait_ge(s_exp, b.c)
                elif b.i is None and b.c == 0:
                    pe.wait_ge(s_w[3], 48)
                for t in range(NT):
                    for c in range(KC):
                        mm = pe.matmul(logits[:, t, :], h2_t[:, c, t, :], wg[:, c, :],
                                       start=(c == 0), stop=(c == KC - 1))
                mm.then_inc(s_pg, 1)

            def counted(t, weights, b, of):
                return pe.matmul(rank[:, t, :, :], weights[:], onehot[:, b.buf(2), of, :, :],
                                 start=False, stop=False, skip_group_check=True)

            def close_ranks(b):
                pe.wait_ge(s_pick, b.times(1, 1))
                counted(0, not_before, b, 0)
                counted(0, ones_bf, b, 1)
                return counted(1, not_before, b, 1)

            def rank_tokens(b):
                pe.wait_ge(s_oh, b.times(1, 1))
                if b.i is not None or b.c >= 1:
                    close_ranks(b - 1)
                counted(0, before, b, 0)
                counted(1, ones_bf, b, 0)
                counted(1, before, b, 1).then_inc(s_prk, 1)

            def step(s):
                if s.exists():
                    project_kv(s)
                if (s - 1).exists():
                    attend(s - 1)
                if s.exists():
                    transpose_h(s)
                    multiply_ktv(s)
                    project_q(s, 0)
                if (s - 3).exists():
                    rank_tokens(s - 3)
                if (s - 2).exists():
                    transpose_h2(s - 2)
                if s.exists():
                    project_q(s, 1)
                if (s - 2).exists():
                    gate(s - 2)

            dense_steps(pe, step, 0, NB + 3)
            close_ranks(Batch(None, NB - 1)).then_inc(s_end, 1)

            pe.wait_ge(s_found, 1)
            pe.transpose(ps_kv[0:8, 0:P], found[:].rearrange("p q c h -> p (q c h)"), ident[:]).then_inc(s_tt, 1)

            def transpose_rows(j, count, wait):
                pe.wait_ge(s_in[j], wait)
                if not (isinstance(count, int) and count < 2):
                    pe.wait_ge(s_rt, count - 1)
                for c in range(KC):
                    mm = pe.transpose(ps_rt[j % 2][:, c, 0, :], row_in[:, j, c * P:(c + 1) * P], ident[:])
                mm.then_inc(s_prt, 1)

            trips = TILES // V

            def multiply(k, j, i):
                at = pe.value_load(table[0:1, 1, k, bass.ds(i * V + j, 1)], min_val=0, max_val=(E - 1) * D)
                count = i * V + (k * TILES + j)
                last = isinstance(i, int) and k == 1 and i == trips - 1 and j == V - 1
                if not last:
                    jn = (j + 1) % V
                    transpose_rows(jn, i * V + (k * TILES + j + 1), i * 16 + 16 * (k * trips + 1 + (j + 1) // V))
                pe.wait_ge(s_rt, i * V + (k * TILES + j + 1))
                if not (isinstance(i, int) and k == 0 and i == 0 and j < 2):
                    pe.wait_ge(s_y, i * V + (k * TILES + j - 1))
                o = ps_y[j % 2]
                for c in range(KC):
                    pe.matmul(o, row_t[:, j % 2, c, :], we[:, c, bass.ds(at, D)], start=(c == 0), stop=False)
                pe.matmul(o, ones_bf[:], be_rows[:, bass.ds(at, D)], start=False, stop=True).then_inc(s_py, 1)

            pe.wait_ge(s_table, 16)
            pe.wait_ge(s_w[4], 16)
            pe.wait_ge(s_eb, 16)
            transpose_rows(0, 0, 16)
            expert_steps(pe, multiply, 0, peel_first=True)
            expert_steps(pe, multiply, 1, peel_last=True)

        @block.scalar
        def _(act):
            act.add_instruction(mybir.InstLoadActFuncSet(name=nc.get_next_instruction_name(),
                                                         act_func_set_id=LOG_EXP_SET, ins=[], outs=[]))
            act.wait_ge(s_zero, 2)

            def inverse_root(n, b):
                act.wait_ge(s_mv[n], b.times(1, 1))
                act.activation(lnv[:, n, :], mv[:, n, b.buf(2), :, 1], ACT.Ln, bias=eps[:, 0:1]).then_inc(s_ln[n], 1)
                act.wait_ge(s_ln[n], b.times(1, 1))
                act.activation(rstd[:, n, b.buf(2), :], lnv[:, n, :], ACT.Exp, scale=-0.5).then_inc(s_rstd[n], 1)

            def copy_q(b, dc):
                act.wait_ge(s_pq, b.times(2, dc + 1))
                if dc == 0 and (b.i is not None or b.c >= 1):
                    act.wait_ge(s_patt, (b - 1).times(1, 1))
                if b.i is None and b.c == 0:
                    act.wait_ge(s_w[2], 32)
                act.activation(q_t[:, dc, :, :].rearrange("p t n -> p (t n)"), ps_q[dc][:, 0:S], ACT.Identity,
                               bias=bq_sb[:, dc:dc + 1]).then_inc(s_q, 1)

            def gate_exps(b):
                act.wait_ge(s_gap, b.times(1, 1))
                if b.i is not None or b.c >= 1:
                    act.wait_ge(s_w1, (b - 1).times(1, 1))
                for t in range(NT):
                    act.activation(exps[:, t, :], logits[:, t, :], ACT.Exp, bias=neg_max[:, t:t + 1],
                                   accum_out=sums[:, t:t + 1])
                act.activation(exp_gap[:], gap[:], ACT.Exp).then_inc(s_exp, 1)

            def normalise_h2(b):
                act.wait_ge(s_nmr[2], b.times(1, 1))
                if b.i is not None or b.c >= 4:
                    act.wait_ge(s_row[b.buf(4)], (b - 4).uses(4, 64))
                for t in range(NT):
                    a = act.activation(rows[:, b.buf(4), t, 0:D], x1[:, b.buf(2), t, :], ACT.Identity,
                                       bias=nmr[:, 2, t:t + 1], scale=rstd[:, 2, b.buf(2), t:t + 1])
                a.then_inc(s_h2, 1)

            def copy_kv(b):
                act.wait_ge(s_pkv, b.times(1, 1))
                if b.i is not None or b.c >= 1:
                    act.wait_ge(s_pm, (b - 1).times(1, 1))
                act.activation(kv[:].rearrange("p a d -> p (a d)"), ps_kv[0:SC, :], ACT.Copy).then_inc(s_kv, 1)

            def normalise_x(b):
                act.wait_ge(s_nmr[0], b.times(1, 1))
                if b.i is not None or b.c >= 4:
                    act.wait_ge(s_att, (b - 4).times(1, 1))
                    act.wait_ge(s_pht, (b - 4).times(1, 1))
                for t in range(NT):
                    a = act.activation(h[:, b.buf(4), t, :], x_sb[:, b.buf(4), t, :], ACT.Identity,
                                       bias=nmr[:, 0, t:t + 1], scale=rstd[:, 0, b.buf(2), t:t + 1])
                a.then_inc(s_h, 1)

            def copy_h_t(b):
                act.wait_ge(s_pht, b.times(1, 1))
                if b.i is not None or b.c >= 1:
                    act.wait_ge(s_pq, (b - 1).times(2, 2))
                act.activation(h_t[:], ps_ht[:], ACT.Copy).then_inc(s_ht, 1)

            def copy_h2_t(b):
                act.wait_ge(s_ph2t, b.times(1, 1))
                if b.i is not None or b.c >= 1:
                    act.wait_ge(s_pg, (b - 1).times(1, 1))
                act.activation(h2_t[:], ps_h2t[:], ACT.Copy).then_inc(s_h2t, 1)

            def step(s):
                p, b, f, nxt = s - 1, s - 2, s - 3, s + 1
                if p.exists():
                    copy_q(p, 1)
                if b.exists():
                    inverse_root(2, b)
                if f.exists():
                    gate_exps(f)
                if s.exists():
                    copy_kv(s)
                if nxt.exists():
                    inverse_root(0, nxt)
                if s.exists():
                    copy_h_t(s)
                if b.exists():
                    normalise_h2(b)
                if p.exists():
                    inverse_root(1, p)
                if s.exists():
                    copy_q(s, 0)
                if b.exists():
                    copy_h2_t(b)
                if nxt.exists():
                    normalise_x(nxt)

            dense_steps(act, step, -1, NB + 3)

            def weigh(k, j, i):
                act.wait_ge(s_py, i * V + (k * TILES + j + 1))
                if not (isinstance(i, int) and k == 0):
                    act.wait_ge(s_add[j], i * 16 + 16 * k * (TILES // V))
                act.activation(y[:, j, :], ps_y[j % 2], ACT.Relu,
                               scale=row_in[:, j, W_COL + k:W_COL + k + 1]).then_inc(s_y, 1)

            for k in range(2):
                expert_steps(act, weigh, k, peel_first=(k == 0))

        @block.vector
        def _(dve):
            dve.memset(zeros[:], 0.0).then_inc(s_zero, 1)
            dve.memset(eps[:], EPS).then_inc(s_zero, 1)
            dve.memset(bkv_rows[:].bitcast(U32), 0)
            dve.memset(be_rows[:].bitcast(U32), 0).then_inc(s_zero, 1)

            def split(src, rest, part, n):
                dve.tensor_copy(part[:, 0, :], src).then_inc(s_split, 1)
                dve.wait_ge(s_split, n + 1)
                dve.tensor_tensor(rest[:, 0, :], src, part[:, 0, :], ALU.subtract).then_inc(s_split, 1)
                dve.wait_ge(s_split, n + 2)
                dve.tensor_copy(part[:, 1, :], rest[:, 0, :]).then_inc(s_split, 1)
                dve.wait_ge(s_split, n + 3)
                dve.tensor_tensor(rest[:, 1, :], rest[:, 0, :], part[:, 1, :], ALU.subtract).then_inc(s_split, 1)
                dve.wait_ge(s_split, n + 4)
                dve.tensor_copy(part[:, 2, :], rest[:, 1, :]).then_inc(s_split, 1)

            def stats(n, b, src):
                for t in range(NT):
                    i = dve.bn_stats(st[:, n, t, :], src[:, t, :])
                i.then_inc(s_st[n], 1)

            def moments(n, b):
                dve.wait_ge(s_st[n], b.times(1, 1))
                settle(dve, s_passed[0])
                for t in range(NT):
                    i = dve.bn_aggr(mv[:, n, b.buf(2), t, :], st[:, n, t, :])
                i.then_inc(s_mv[n], 1)

            def mean_shift(n, b):
                dve.wait_ge(s_rstd[n], b.times(1, 1))
                dve.scalar_tensor_tensor(out=nmr[:, n, :], in0=mv[:, n, b.buf(2), :, 0], scalar=-1.0,
                                         in1=rstd[:, n, b.buf(2), :], op0=ALU.mult,
                                         op1=ALU.mult).then_inc(s_nmr[n], 1)

            def step(s):
                p, b, f, nxt = s - 1, s - 2, s - 3, s + 1
                if b.exists():
                    dve.wait_ge(s_x1, b.times(1, 1))
                    stats(2, b, x1[:, b.buf(2)])
                if f.exists():
                    dve.wait_ge(s_pg, f.times(1, 1))
                    settle(dve, s_passed[0])
                    for t in range(NT):
                        i = dve.max(top[:, t, :], logits[:, t, :])
                    i.then_inc(s_top, 1)
                if b.exists():
                    moments(2, b)
                if f.exists():
                    dve.wait_ge(s_top, f.times(1, 1))
                    settle(dve, s_passed[0])
                    for t in range(NT):
                        i = dve.max_index(top_i[:, t, :], top[:, t, :], logits[:, t, :])
                    i.then_inc(s_topi, 1)
                    dve.tensor_scalar(neg_max[:], top[:, :, 0], -1.0, None, ALU.mult)
                    dve.tensor_tensor(gap[:], top[:, :, 1], top[:, :, 0], ALU.subtract).then_inc(s_gap, 1)
                if nxt.exists():
                    dve.wait_ge(s_x[nxt.buf(4)], nxt.uses(4, 16))
                    if nxt.i is not None or nxt.c >= 1:
                        dve.wait_ge(s_mv[0], (nxt - 1).times(1, 1))
                    stats(0, nxt, x_sb[:, nxt.buf(4)])
                if f.exists():
                    dve.wait_ge(s_topi, f.times(1, 1))
                    dve.tensor_copy(top_f[:], top_i[:, :, 0:2]).then_inc(s_topf, 1)
                if nxt.exists():
                    moments(0, nxt)
                if b.exists():
                    mean_shift(2, b)
                if f.exists():
                    dve.wait_ge(s_topf, f.times(1, 1))
                    dve.tensor_tensor(onehot[:, f.buf(2)].rearrange("p t c e -> p (t c) e"),
                                      iota_e[:].unsqueeze(1).to_broadcast([P, NT * 2, E]),
                                      top_f[:].rearrange("p t c -> p (t c)").unsqueeze(2)
                                      .to_broadcast([P, NT * 2, E]), ALU.is_equal).then_inc(s_oh, 1)
                if f.exists():
                    dve.wait_ge(s_exp, f.times(1, 1))
                    dve.reciprocal(rows[:, f.buf(4), :, W_COL], sums[:]).then_inc(s_w0, 1)
                    ids = rows[:, f.buf(4), :, ID_COL].bitcast(I32)
                    if f.i is not None or f.c >= 4:
                        dve.tensor_scalar(ids, ids, 4 * S, None, ALU.add).then_inc(s_id, 1)
                    else:
                        dve.sem_inc(s_id, 1)
                if p.exists():
                    dve.wait_ge(s_patt, p.times(1, 1))
                    dve.wait_ge(s_h, p.times(1, 1))
                    dve.tensor_tensor(att[:], ps_att[:], h[:, p.buf(4)], ALU.add).then_inc(s_att, 1)
                if f.exists():
                    dve.wait_ge(s_w0, f.times(1, 1))
                    dve.tensor_tensor(rows[:, f.buf(4), :, W_COL + 1], rows[:, f.buf(4), :, W_COL], exp_gap[:],
                                      ALU.mult).then_inc(s_w1, 1)
                if p.exists():
                    dve.wait_ge(s_att, p.times(1, 1))
                    stats(1, p, att)
                if nxt.exists():
                    mean_shift(0, nxt)
                if s.exists():
                    dve.wait_ge(s_pm, s.times(1, 1))
                    if s.i is not None or s.c >= 1:
                        dve.wait_ge(s_patt, (s - 1).times(1, 1))
                    dve.tensor_tensor(kvm[:].rearrange("p c n -> p (c n)"), ktv,
                                      head_mask[:].rearrange("p c n -> p (c n)"), ALU.mult).then_inc(s_m, 1)
                if p.exists():
                    moments(1, p)
                if f.exists():
                    dve.wait_ge(s_prk, f.times(1, 1))
                    dve.tensor_tensor(picked[:], rank.rearrange("p t c e -> p (t c) e"),
                                      onehot[:, f.buf(2)].rearrange("p t c e -> p (t c) e"),
                                      ALU.mult).then_inc(s_pick, 1)
                if p.exists():
                    dve.wait_ge(s_mv[1], p.times(1, 1))
                    for t in range(NT):
                        i = dve.scalar_tensor_tensor(out=scaled[:, t, :], in0=att[:, t, :],
                                                     scalar=mv[:, 1, p.buf(2), t, 0:1], in1=gamma_sb[:],
                                                     op0=ALU.subtract, op1=ALU.mult)
                    i.then_inc(s_scaled, 1)
                if f.exists():
                    dve.wait_ge(s_pick, f.times(1, 1))
                    dve.tensor_reduce(signed_pos[:], picked[:], AX_X, ALU.add).then_inc(s_sum, 1)
                if p.exists():
                    dve.wait_ge(s_scaled, p.times(1, 1))
                    dve.wait_ge(s_rstd[1], p.times(1, 1))
                    dve.wait_ge(s_xb, p.times(1, 1))
                    if p.i is not None or p.c >= 2:
                        dve.wait_ge(s_h2, (p - 2).times(1, 1))
                        dve.wait_ge(s_x1w[p.buf(2)], (p - 2).uses(2, 16))
                    for t in range(NT):
                        i = dve.scalar_tensor_tensor(out=x1[:, p.buf(2), t, :], in0=scaled[:, t, :],
                                                     scalar=rstd[:, 1, p.buf(2), t:t + 1],
                                                     in1=x_beta[:, p.buf(2), t, :], op0=ALU.mult, op1=ALU.add)
                    i.then_inc(s_x1, 1)
                if f.exists():
                    dve.wait_ge(s_sum, f.times(1, 1))
                    if f.i is not None or f.c >= 2:
                        dve.wait_ge(s_row[(f - 2).buf(4)], (f - 2).uses(4, 64))
                    dve.scalar_tensor_tensor(out=pos[:, f.buf(2)].rearrange("p t c -> p (t c)"),
                                             in0=signed_pos[:], scalar=-1.0, in1=signed_pos[:],
                                             op0=ALU.mult, op1=ALU.max).then_inc(s_pos, 1)

            dve.wait_ge(s_w[1], 16)
            split(bkv_in[:], bkv_rest, bkv_part, 0)
            dve.wait_ge(s_be_in, 16)
            split(be_in[:], be_rest, be_part, 5)
            dve.wait_ge(s_const, 1)
            dve.wait_ge(s_w[3], 48)
            dense_steps(dve, step, -1, NB + 3)

            steps = [0]

            def done(ins):
                steps[0] += 1
                ins.then_inc(s_tab, 1)
                dve.wait_ge(s_tab, steps[0])

            base0 = bin_base[:, 0]
            dve.wait_ge(s_end, 1)
            done(dve.tensor_copy(ends[:], rank[:, 0]))
            pairs = ends[:].rearrange("p c (r o) -> p c r o", o=2)
            pad_pairs = pad_at[:].rearrange("p c (r o) -> p c r o", o=2)
            dve.tensor_copy(pad_pairs[:, :, :, 0], pairs[:, :, :, 0])
            dve.tensor_scalar(pad_pairs[:, :, :, 1], pairs[:, :, :, 1], -1.0, float(1 - P), ALU.mult,
                              ALU.add).then_inc(s_pad, 1)
            done(dve.tensor_tensor(counts[:], ends[:], base0, ALU.subtract))
            done(dve.tensor_scalar(cnt_i[:], counts[:], float(P - 1), None, ALU.add))
            done(dve.tensor_scalar(tiles_i[:], cnt_i[:], P.bit_length() - 1, None, ALU.logical_shift_right))
            done(dve.tensor_copy(tiles_f[:], tiles_i[:]))
            done(dve.tensor_copy(scan[:, 0], tiles_f[:]))
            a, d = 0, 1
            while d < E:
                done(dve.tensor_copy(scan[:, 1 - a, :, 0:d], scan[:, a, :, 0:d]))
                done(dve.tensor_tensor(scan[:, 1 - a, :, d:E], scan[:, a, :, d:E], scan[:, a, :, 0:E - d],
                                       ALU.add))
                a, d = 1 - a, 2 * d
            upto = scan[:, a]
            before_e = scan[:, 1 - a]
            done(dve.tensor_tensor(before_e, upto, tiles_f[:], ALU.subtract))
            sh = shift[:, :, 0:E].rearrange("p c (r o) -> p c r o", o=2)
            bp = base0.rearrange("p c (r o) -> p c r o", o=2)
            tp = tiles_f[:].rearrange("p c (r o) -> p c r o", o=2)
            done(dve.tensor_copy(sh[:, :, :, 0], bp[:, :, :, 0]))
            for k in range(2):
                done(dve.scalar_tensor_tensor(out=sh[:, k, :, 1], in0=tp[:, k, :, 1], scalar=float(P),
                                              in1=bp[:, k, :, 1], op0=ALU.mult, op1=ALU.add))
            done(dve.tensor_scalar(sh[:, :, :, 1], sh[:, :, :, 1], -1.0, 1.0, ALU.mult, ALU.add))
            done(dve.scalar_tensor_tensor(out=shift[:, :, 0:E], in0=before_e, scalar=-float(P),
                                          in1=shift[:, :, 0:E], op0=ALU.mult, op1=ALU.add))
            done(dve.tensor_scalar(shift[:, :, E], upto[:, :, E - 1], -float(P), float(SPARE), ALU.mult, ALU.add))
            done(dve.tensor_tensor(delta[:], shift[:, :, 1:E + 1], shift[:, :, 0:E], ALU.subtract))
            for k in range(2):
                done(dve.tensor_tensor(reached[:, k], tile_no[:].unsqueeze(2).to_broadcast([P, 2, E]),
                                       upto[:, k].unsqueeze(1).to_broadcast([P, 2, E]), ALU.is_ge))
                done(dve.tensor_tensor(reached_d[:, k], reached[:, k],
                                       delta[:, k].unsqueeze(1).to_broadcast([P, 2, E]), ALU.mult))
                done(dve.tensor_reduce(found[:, 0, k, :], reached_d[:, k], AX_X, ALU.add))
                done(dve.tensor_reduce(found[:, 1, k, :], reached[:, k], AX_X, ALU.add))
                done(dve.tensor_scalar(found[:, 0, k, :], found[:, 0, k, :], shift[:, k, 0:1], None, ALU.add))
                done(dve.scalar_tensor_tensor(out=found[:, 0, k, :], in0=tile_no[:], scalar=float(P),
                                              in1=found[:, 0, k, :], op0=ALU.mult, op1=ALU.add))
            dve.tensor_scalar(found[:, 1], found[:, 1], float(E - 1), float(D), ALU.min,
                              ALU.mult).then_inc(s_found, 1)
            dve.wait_ge(s_tt, 1)
            dve.tensor_copy(table8[:], ps_kv[0:8, 0:P]).then_inc(s_t8, 1)

            def copy_rows(k, j, i):
                dve.wait_ge(s_prt, i * V + (k * TILES + j + 1))
                if not (isinstance(i, int) and k == 0 and j < 2):
                    dve.wait_ge(s_py, i * V + (k * TILES + j - 1))
                dve.tensor_copy(row_t[:, j % 2], ps_rt[j % 2][:, :, 0, :]).then_inc(s_rt, 1)

            for k in range(2):
                expert_steps(dve, copy_rows, k, peel_first=(k == 0))


def kernel(**inputs):
    import numpy as np
    import concourse.bacc as bacc
    from concourse.bass_utils import run_bass_kernel_spmd

    g = {n.replace("L0_xattn_", "").replace("L0_ffn_", ""): np.asarray(v) for n, v in inputs.items()}
    c = np.ascontiguousarray
    arrays = {
        "x": c(g["x"].reshape(TOK, D)),
        "ctx_t": c(g["ctx_1024"].transpose(0, 2, 1).reshape(NB, KC, P, SC).transpose(0, 2, 1, 3)),
        "wkv_t": c(np.concatenate([g["Wk"].T, g["Wv"].T], axis=1)),
        "wq_t": c(g["Wq"].T),
        "gate_t": c(g["gate_w"].T),
        "we_t": c(g["expert_w"].transpose(2, 0, 1).reshape(D, E * D)),
        "bkv": c(np.concatenate([g["bk"], g["bv"]])),
        "be": c(g["expert_b"].reshape(E * D)),
        "bq": c(g["bq"].reshape(KC, P).T),
        "gamma": c(g["ln_gamma"]),
        "beta": c(g["ln_beta"]),
    }
    nc = bacc.Bacc("TRN2", target_bir_lowering=False, num_devices=1)
    args = [nc.dram_tensor(f"in_{n}", a.shape, mybir.dt.from_np(a.dtype), kind="ExternalInput").ap()
            for n, a in arrays.items()]
    out = nc.dram_tensor("out_rows", (OUT_ROWS, D), F32, kind="ExternalOutput").ap()
    build(nc, *args, out)
    r = run_bass_kernel_spmd(nc, [{f"in_{n}": a for n, a in arrays.items()}], core_ids=[0])
    return r.results[0]["out_rows"][0:TOK].reshape(NB, S, D)
```

```python
from contextlib import ExitStack

import concourse.bass as bass
from concourse import mybir

F32 = mybir.dt.float32
BF16 = mybir.dt.bfloat16
I32 = mybir.dt.int32
U32 = mybir.dt.uint32
ALU = mybir.AluOpType
ACT = mybir.ActivationFunctionType
AX_X = mybir.AxisListType.X

P = 128
NB, S, D = 64, 256, 256
SC = 120
NH = 16
E = 16
NT = S // P
KC = D // P
TOK = NB * S
SCALE = (D // NH) ** -0.5
EPS = 1e-5

ROW = D + 4
W_COL, ID_COL = D, D + 2
PAD = P
REGION = TOK + 2 * PAD
TILES = TOK // P + E
SPARE = E // 2 * REGION
ROWS = SPARE + E * P
PAD_ID = TOK
OUT_ROWS = TOK + 2 * E * P

U = 4
LEAD, LOOPS = 12, (NB - 4 - 12) // U
V = 12
PAIRS = V // 2
TRIPS = TILES // V
WE_PIECES = 8
TAILS = 2 * E // 4
LOG_EXP_SET = 6


class Batch:

    def __init__(self, i, c):
        self.i, self.c = i, c

    def __sub__(self, n):
        return Batch(self.i, self.c - n)

    def __add__(self, n):
        return Batch(self.i, self.c + n)

    def exists(self, low=0):
        return self.i is not None or low <= self.c < NB

    def times(self, k, plus=0):
        n = k * self.c + plus
        return n if self.i is None else self.i * (k * U) + n

    def uses(self, bufs, k):
        n = k * (self.c // bufs + 1)
        return n if self.i is None else self.i * (k * U // bufs) + n

    def buf(self, bufs):
        return self.c % bufs


def settle(eng, passed):
    eng.sem_inc(passed, 1)


def dense_steps(eng, step, low, high):
    for s in range(low, LEAD):
        step(Batch(None, s))
    with eng.Fori(0, LOOPS) as i:
        for j in range(U):
            step(Batch(i, LEAD + j))
    for s in range(LEAD + LOOPS * U, high):
        step(Batch(None, s))


def expert_bodies(eng, body, k, peel_first=False, peel_last=False):
    if peel_first:
        body(k, 0)
    with eng.Fori(int(peel_first), TRIPS - int(peel_last)) as i:
        body(k, i)
    if peel_last:
        body(k, TRIPS - 1)


def load_values(nc, eng, name, source, count, max_val):
    regs = [eng.alloc_register(f"{name}{n}") for n in range(count)]

    def load(at):
        eng.load(regs, source(at))
        return [nc.snap(r, min_val=0, max_val=max_val) for r in regs]

    return load


def build(nc, x, ctx_t, wkv_t, wq_t, gate_t, we_t, bkv, be, bq, gamma, beta, out):
    bins = [nc.dram_tensor(f"bins{k}", [ROWS, ROW], F32, kind="Internal").ap() for k in range(2)]
    bkv_dram = nc.dram_tensor("bkv_dram", [3, 2 * D], BF16, kind="Internal").ap()
    be_dram = nc.dram_tensor("be_dram", [3, E * D], BF16, kind="Internal").ap()

    def parts_as_rows(dram):
        return dram.rearrange("n (p m) -> p n m", p=P)

    with ExitStack() as ctx:
        def sb(name, shape, dt=F32):
            return ctx.enter_context(nc.sbuf_tensor(name, shape, dt))

        def ps(name, shape, dt=F32):
            return ctx.enter_context(nc.psum_tensor(name, shape, dt))

        def sem(name):
            return ctx.enter_context(nc.semaphore(name))

        ident = sb("ident", [P, P])
        ones_row = sb("ones_row", [1, P])
        ones_bf = sb("ones_bf", [P, P], BF16)
        before = sb("before", [P, P], BF16)
        not_before = sb("not_before", [P, P], BF16)
        head_mask = sb("head_mask", [P, KC, P])
        iota_e = sb("iota_e", [P, E])
        tile_no = sb("tile_no", [P, 2])
        bin_base = sb("bin_base", [P, NT, 2, E])
        eps = sb("eps", [P, 1])
        wkv = sb("wkv", [P, KC, 2 * D])
        wq = sb("wq", [P, KC, D])
        wg = sb("wg", [P, KC, E])
        we = sb("we", [P, KC, E * D])
        bkv_rows = sb("bkv_rows", [P, 2 * D], BF16)
        be_rows = sb("be_rows", [P, E * D], BF16)
        bkv_in = sb("bkv_in", [P, 2 * D // P])
        be_in = sb("be_in", [P, E * D // P])
        bkv_rest = sb("bkv_rest", [P, 2, 2 * D // P])
        be_rest = sb("be_rest", [P, 2, E * D // P])
        bkv_part = sb("bkv_part", [P, 3, 2 * D // P], BF16)
        be_part = sb("be_part", [P, 3, E * D // P], BF16)
        bq_sb = sb("bq_sb", [P, KC])
        gamma_sb = sb("gamma_sb", [P, D])
        beta_sb = sb("beta_sb", [P, D])
        zeros = sb("zeros", [P, 4 * D])
        pad_rows = sb("pad_rows", [P, E, ROW])
        spare_rows = sb("spare_rows", [P, E, ROW])

        x_sb = sb("x_sb", [P, 4, NT, D])
        c_sb = sb("c_sb", [P, 4, KC, SC])
        h = sb("h", [P, 4, NT, D])
        h_t = sb("h_t", [P, KC, NT, P])
        kv = sb("kv", [SC, 2, D])
        q_t = sb("q_t", [P, KC, NT, P])
        kvm = sb("kvm", [P, KC, P])
        att = sb("att", [P, NT, D])
        scaled = sb("scaled", [P, NT, D])
        x_beta = sb("x_beta", [P, 2, NT, D])
        x1 = sb("x1", [P, 2, NT, D])
        rows = sb("rows", [P, 4, NT, ROW])
        h2_t = sb("h2_t", [P, KC, NT, P])
        st = sb("st", [P, 3, NT, 6])
        mv = sb("mv", [P, 3, 2, NT, 2])
        lnv = sb("lnv", [P, 3, NT])
        rstd = sb("rstd", [P, 3, 2, NT])
        nmr = sb("nmr", [P, 3, NT])
        scores = sb("scores", [P, NT, E])
        top = sb("top", [P, NT, 8])
        top_i = sb("top_i", [P, NT, 8], U32)
        top_f = sb("top_f", [P, NT, 2])
        neg_max = sb("neg_max", [P, NT])
        gap = sb("gap", [P, NT])
        exps = sb("exps", [P, NT, E])
        sums = sb("sums", [P, NT])
        exp_gap = sb("exp_gap", [P, NT])
        onehot = sb("onehot", [P, 2, NT, 2, E], BF16)
        picked = sb("picked", [P, NT * 2, E])
        signed_pos = sb("signed_pos", [P, NT * 2])
        pos = sb("pos", [P, 2, NT, 2], I32)

        ends = sb("ends", [P, 2, E])
        counts = sb("counts", [P, 2, E])
        pad_at = sb("pad_at", [P, 2, E], I32)
        cnt_i = sb("cnt_i", [P, 2, E], I32)
        tiles_i = sb("tiles_i", [P, 2, E], I32)
        tiles_f = sb("tiles_f", [P, 2, E])
        scan = sb("scan", [P, 2, 2, E])
        shift = sb("shift", [P, 2, E + 1])
        delta = sb("delta", [P, 2, E])
        reached = sb("reached", [P, 2, 2, E])
        reached_d = sb("reached_d", [P, 2, 2, E])
        found = sb("found", [P, 2, 2, 2])
        table = sb("table", [1, 2, 2, 2 * P], I32)

        row_in = sb("row_in", [P, V, ROW])
        row_t = sb("row_t", [P, 2, 2, KC, P])
        y = sb("y", [P, V, D])

        ps_ht = ps("ps_ht", [P, KC, NT, P])
        ps_kv = ps("ps_kv", [P, 2 * D])
        ps_q = [ps(f"ps_q{n}", [P, 512]) for n in range(KC)]
        ps_mg = ps("ps_mg", [P, 512])
        ps_att = ps("ps_att", [P, NT, D])
        ps_h2t = ps("ps_h2t", [P, KC, NT, P])
        ps_rank = ps("ps_rank", [P, 512])
        ktv = ps_mg[:, 0:D]
        logits = ps_mg[:, D:D + NT * E].rearrange("p (t e) -> p t e", e=E)
        rank = ps_rank[:, 0:NT * 2 * E].rearrange("p (t c e) -> p t c e", t=NT, e=E)
        ps_rt = [ps_ht, ps_h2t]
        ps_y = [ps_att] + [ps_q[n][:].rearrange("p (t d) -> p t d", t=2) for n in range(2)]
        ps_table = [ps_kv, ps_q[0]]

        s_w = [sem(f"weights{n}_loaded") for n in range(4)]
        s_we = sem("expert_weights_loaded")
        s_be_in = sem("expert_bias_loaded")
        s_const = sem("pool_constants_made")
        s_step = sem("pool_step_done")
        s_passed = [sem(f"passed_by_{n}") for n in ("dve", "pool")]
        s_zero = sem("zeros_made")
        s_split = sem("bias_split_step")
        s_kvb = sem("kv_bias_rows_placed")
        s_eb = sem("expert_bias_rows_placed")
        s_kvd = sem("kv_bias_parts_in_dram")
        s_ebd = sem("expert_bias_parts_in_dram")
        s_init = sem("dram_fill_written")
        s_rank0 = sem("rank_started")
        s_x = [sem(f"x_loaded{n}") for n in range(4)]
        s_c = [sem(f"context_loaded{n}") for n in range(4)]
        s_x1w = [sem(f"x1_written{n}") for n in range(2)]
        s_row = [sem(f"rows_scattered{n}") for n in range(4)]
        s_st = [sem(f"stats{n}_ready") for n in range(3)]
        s_mv = [sem(f"moments{n}_ready") for n in range(3)]
        s_ln = [sem(f"log_var{n}_ready") for n in range(3)]
        s_rstd = [sem(f"rstd{n}_ready") for n in range(3)]
        s_nmr = {0: sem("shift0_ready"), 2: sem("shift2_ready")}
        s_h = sem("h_ready")
        s_pht = sem("h_transposed")
        s_ht = sem("h_t_copied")
        s_pkv = sem("kv_projected")
        s_kv = sem("kv_copied")
        s_pq = sem("q_projected")
        s_q = sem("q_copied")
        s_pm = sem("ktv_multiplied")
        s_m = sem("ktv_masked")
        s_patt = sem("attention_multiplied")
        s_att = sem("attention_residual_ready")
        s_scaled = sem("scaled_ready")
        s_xb = sem("x_beta_ready")
        s_x1 = sem("x1_ready")
        s_h2 = sem("h2_ready")
        s_ph2t = sem("h2_transposed")
        s_h2t = sem("h2_t_copied")
        s_pg = sem("logits_ready")
        s_sc = sem("scores_copied")
        s_top = sem("top_values_ready")
        s_topi = sem("top_indices_ready")
        s_gap = sem("gap_ready")
        s_topf = sem("indices_as_floats")
        s_oh = sem("onehot_ready")
        s_exp = sem("exps_ready")
        s_w0 = sem("first_weight_ready")
        s_w1 = sem("second_weight_ready")
        s_id = sem("ids_advanced")
        s_prk = sem("ranks_ready")
        s_pick = sem("rank_picked")
        s_sum = sem("signed_position_ready")
        s_pos = sem("positions_ready")
        s_end = sem("rank_ends_ready")
        s_pad = sem("pad_positions_ready")
        s_padw = [sem(f"pad_rows_written{k}") for k in range(2)]
        s_tab = sem("table_step")
        s_found = sem("table_columns_ready")
        s_tt = sem("table_transposed")
        s_table = sem("table_placed")
        s_in = [sem(f"row_pair_loaded{n}") for n in range(PAIRS)]
        s_prt = sem("row_pair_transposed")
        s_rt = sem("row_pair_copied")
        s_py = sem("pair_multiplied")
        s_y = sem("pair_result_ready")
        s_add = [sem(f"pair_result_added{n}") for n in range(PAIRS)]

        x_v = x.rearrange("(n p t) d -> n p t d", p=P, t=NT)
        out_v = out[0:TOK, :].rearrange("(n p t) d -> n p t d", p=P, t=NT)

        def batch_of(view, b):
            if b.i is None:
                return view[b.c]
            return view[bass.ds(b.times(1), 1)].rearrange("o p a d -> (o p) a d")

        def bin_ends(eng, k, low, high):
            eng.wait_ge(s_pad, 1)
            load = load_values(nc, eng, f"pad{k}_", lambda at: pad_at[0:1, k, low:high], high - low, SPARE - P)
            return {low + n: at for n, at in enumerate(load(0))}

        def fill(eng, k, ends):
            for e, at in ends.items():
                eng.dma_start(bins[k][bass.ds(at, P), :], pad_rows[:, e, :]).then_inc(s_padw[k], 16)

        block = ctx.enter_context(nc.Block())

        @block.sync
        def _(sp):
            def load(b):
                n = b.buf(4)
                if b.i is not None or b.c >= 4:
                    sp.wait_ge(s_xb, (b - 4).times(1, 1))
                    sp.wait_ge(s_h, (b - 4).times(1, 1))
                    sp.wait_ge(s_pkv, (b - 4).times(1, 1))
                sp.dma_start(x_sb[:, n], batch_of(x_v, b)).then_inc(s_x[n], 16)
                sp.dma_start(c_sb[:, n], batch_of(ctx_t, b)).then_inc(s_c[n], 16)

            load(Batch(None, 0))
            sp.dma_start(bkv_in[:], bkv.rearrange("(p n) -> p n", p=P)).then_inc(s_w[1], 16)
            sp.dma_start(wkv[:], wkv_t.rearrange("(c p) n -> p c n", p=P)).then_inc(s_w[0], 16)
            sp.dma_start(wq[:], wq_t.rearrange("(c p) n -> p c n", p=P)).then_inc(s_w[2], 16)
            sp.dma_start(bq_sb[:], bq).then_inc(s_w[2], 16)
            sp.dma_start(beta_sb[:], beta.partition_broadcast(P)).then_inc(s_w[3], 16)
            sp.dma_start(gamma_sb[:], gamma.partition_broadcast(P)).then_inc(s_w[3], 16)
            sp.dma_start(wg[:], gate_t.rearrange("(c p) n -> p c n", p=P)).then_inc(s_w[3], 16)
            load(Batch(None, 1))
            sp.wait_ge(s_split, 5)
            sp.dma_start(parts_as_rows(bkv_dram), bkv_part[:]).then_inc(s_kvd, 16)
            load(Batch(None, 2))
            sp.wait_ge(s_kvd, 16)
            sp.wait_ge(s_zero, 2)
            sp.dma_start(bkv_rows[0:65:32, :], bkv_dram).then_inc(s_kvb, 16)
            load(Batch(None, 3))
            sp.dma_start(be_in[:], be.rearrange("(p n) -> p n", p=P)).then_inc(s_be_in, 16)

            def prepare_experts(step):
                if step == 2:
                    sp.wait_ge(s_split, 10)
                    sp.dma_start(parts_as_rows(be_dram), be_part[:]).then_inc(s_ebd, 16)
                if step == 3:
                    sp.wait_ge(s_zero, 4)
                    sp.wait_ge(s_ebd, 16)
                    sp.dma_start(be_rows[0:65:32, :], be_dram).then_inc(s_eb, 16)
                if step < TAILS:
                    sp.wait_ge(s_zero, 3)
                    tail = out[TOK:OUT_ROWS, :].rearrange("(n p a) d -> n p (a d)", p=P, a=4)
                    sp.dma_start(tail[step], zeros[:]).then_inc(s_init, 16)
                if step < WE_PIECES:
                    cols = slice(step * E * D // WE_PIECES, (step + 1) * E * D // WE_PIECES)
                    sp.dma_start(we[:, :, cols],
                                 we_t.rearrange("(c p) n -> p c n", p=P)[:, :, cols]).then_inc(s_we, 16)
                if step >= LEAD - 8:
                    q, k = divmod(step - (LEAD - 8), 2)
                    sp.wait_ge(s_const, 2)
                    sp.dma_start(bins[k][SPARE + 4 * q * P:SPARE + 4 * (q + 1) * P, :]
                                 .rearrange("(j p) d -> p j d", p=P),
                                 spare_rows[:, 4 * q:4 * q + 4, :]).then_inc(s_init, 16)

            def step(s):
                p = s - 1
                if p.exists():
                    sp.wait_ge(s_x1, p.times(1, 1))
                    sp.dma_start(batch_of(out_v, p), x1[:, p.buf(2)]).then_inc(s_x1w[p.buf(2)], 16)
                nxt = s + 4
                if nxt.exists():
                    load(nxt)
                if s.i is None and s.c < LEAD:
                    prepare_experts(s.c)

            dense_steps(sp, step, 0, NB + 1)

            fill(sp, 0, bin_ends(sp, 0, 0, E // 2))
            for n in range(4):
                sp.wait_ge(s_row[n], 64 * (NB // 4))
            sp.wait_ge(s_init, 16 * (TAILS + 8))
            sp.wait_ge(s_table, 2)
            first_rows = load_values(nc, sp, "first_row", lambda at: table[0:1, 0, at[0], bass.ds(at[1], V)],
                                     V, ROWS - P)

            def load_rows(k, i):
                firsts = first_rows((k, i * V))
                if isinstance(i, int) and i == 0:
                    sp.wait_ge(s_padw[k], E * 16)
                for j in range(PAIRS):
                    if not (isinstance(i, int) and k == 0):
                        sp.wait_ge(s_add[j], i * 32 + 32 * k * TRIPS)
                    for t in range(2):
                        sp.dma_start(row_in[:, 2 * j + t, :],
                                     bins[k][bass.ds(firsts[2 * j + t], P), :]).then_inc(s_in[j], 16)

            expert_bodies(sp, load_rows, 0, peel_first=True)
            expert_bodies(sp, load_rows, 1, peel_first=True)
            for j in range(PAIRS):
                sp.wait_ge(s_add[j], 2 * 32 * TRIPS)
            for n in range(2):
                sp.wait_ge(s_x1w[n], 16 * (NB // 2))

        @block.gpsimd
        def _(pool):
            steps = [0]

            def done(ins):
                steps[0] += 1
                ins.then_inc(s_step, 1)
                pool.wait_ge(s_step, steps[0])

            done(pool.memset(ident[:], 0.0))
            done(pool.affine_select(out=ident[:], in_=ident[:], compare_op=ALU.not_equal, fill=1.0, base=0,
                                    pattern=[[-1, P]], channel_multiplier=1))
            done(pool.memset(ones_bf[:], 1.0))
            done(pool.memset(ones_row[:], 1.0))
            done(pool.affine_select(out=before[:], in_=ones_bf[:], compare_op=ALU.is_gt, fill=0.0, base=0,
                                    pattern=[[1, P]], channel_multiplier=-1))
            done(pool.affine_select(out=not_before[:], in_=ones_bf[:], compare_op=ALU.is_ge, fill=0.0, base=0,
                                    pattern=[[-1, P]], channel_multiplier=1))
            G = D // NH
            mask = head_mask[:].rearrange("p c (g j) -> p c g j", j=G)
            done(pool.memset(head_mask[:], SCALE))
            done(pool.affine_select(out=mask, in_=mask, compare_op=ALU.is_ge, fill=0.0, base=0,
                                    pattern=[[0, KC], [-G, P // G], [0, G]], channel_multiplier=1))
            done(pool.affine_select(out=mask, in_=mask, compare_op=ALU.is_ge, fill=0.0, base=G - 1,
                                    pattern=[[0, KC], [G, P // G], [0, G]], channel_multiplier=-1))
            done(pool.iota(iota_e[:], [[1, E]], base=0, channel_multiplier=0,
                           allow_small_or_imprecise_dtypes=True))
            done(pool.iota(tile_no[:], [[P, 2]], base=0, channel_multiplier=1,
                           allow_small_or_imprecise_dtypes=True))
            base = bin_base[:].rearrange("p t c (r o) -> p (t c) r o", o=2)
            done(pool.iota(base[:, :, :, 0], [[0, NT * 2], [REGION, E // 2]], base=0, channel_multiplier=0,
                           allow_small_or_imprecise_dtypes=True))
            done(pool.iota(base[:, :, :, 1], [[0, NT * 2], [-REGION, E // 2]], base=1 - REGION,
                           channel_multiplier=0, allow_small_or_imprecise_dtypes=True))
            done(pool.memset(rows[:, :, :, D:ROW], 0.0))
            ids = rows[:].bitcast(I32)[:, :, :, ID_COL]
            pool.iota(ids, [[S, 4], [1, NT]], base=0, channel_multiplier=NT).then_inc(s_const, 1)
            pool.wait_ge(s_w[3], 48)

            def make_pads():
                steps[0] += 1
                pool.wait_ge(s_const, 1)
                pool.memset(pad_rows[:], 0.0)
                pool.memset(spare_rows[:], 0.0).then_inc(s_step, 1)
                pool.wait_ge(s_step, steps[0])
                pool.iota(pad_rows[:].bitcast(I32)[:, :, ID_COL], [[P, E]], base=PAD_ID, channel_multiplier=1)
                pool.iota(spare_rows[:].bitcast(I32)[:, :, ID_COL], [[P, E]], base=PAD_ID + E * P,
                          channel_multiplier=1).then_inc(s_const, 1)

            def step(s):
                if s.exists():
                    n = s.buf(2)
                    pool.wait_ge(s_x[s.buf(4)], s.uses(4, 16))
                    if s.i is not None or s.c >= 2:
                        pool.wait_ge(s_x1, (s - 2).times(1, 1))
                    pool.tensor_tensor(x_beta[:, n], x_sb[:, s.buf(4)],
                                       beta_sb[:].unsqueeze(1).to_broadcast([P, NT, D]),
                                       ALU.add).then_inc(s_xb, 1)
                if s.i is None and s.c == 1:
                    make_pads()
                f = s - 3
                if f.exists():
                    pool.wait_ge(s_w1, f.times(1, 1))
                    pool.wait_ge(s_id, f.times(1, 1))
                    pool.wait_ge(s_pos, f.times(1, 1))
                    settle(pool, s_passed[1])
                    for t in range(NT):
                        for k in range(2):
                            pool.indirect_dma_start(
                                out=bins[k], in_=rows[:, f.buf(4), t, :],
                                out_offset=bass.IndirectOffsetOnAxis(ap=pos[:, f.buf(2), t, k:k + 1], axis=0),
                                in_offset=None).then_inc(s_row[f.buf(4)], 16)

            dense_steps(pool, step, 0, NB + 3)
            for n in range(2):
                pool.wait_ge(s_x1w[n], 16 * (NB // 2))

            def add(k, i):
                for j in range(PAIRS):
                    pool.wait_ge(s_y, i * PAIRS + (k * TRIPS * PAIRS + j + 1))
                    settle(pool, s_passed[1])
                    for t in range(2 * j, 2 * j + 2):
                        pool.indirect_dma_start(
                            out=out, in_=y[:, t, :],
                            out_offset=bass.IndirectOffsetOnAxis(
                                ap=row_in[:, t, ID_COL:ID_COL + 1].bitcast(I32), axis=0),
                            in_offset=None, compute_op=ALU.add).then_inc(s_add[j], 16)

            expert_bodies(pool, add, 0)
            for j in range(PAIRS):
                pool.wait_ge(s_add[j], 32 * TRIPS)
            expert_bodies(pool, add, 1)

        @block.tensor
        def _(pe):
            pe.wait_ge(s_const, 1)
            pe.matmul(ps_rank[:, 0:NT * 2 * E], ones_row[:], bin_base[0:1].rearrange("o t c e -> o (t c e)"),
                      start=True, stop=False, skip_group_check=True).then_inc(s_rank0, 1)

            def project_kv(s):
                n = s.buf(4)
                pe.wait_ge(s_c[n], s.uses(4, 16))
                if s.i is not None or s.c >= 1:
                    pe.wait_ge(s_kv, (s - 1).times(1, 1))
                elif s.c == 0:
                    pe.wait_ge(s_w[0], 16)
                    pe.wait_ge(s_kvb, 16)
                for c in range(KC):
                    pe.matmul(ps_kv[0:SC, :], c_sb[:, n, c, :], wkv[:, c, :], start=(c == 0), stop=False)
                pe.matmul(ps_kv[0:SC, :], ones_bf[:, 0:SC], bkv_rows[:], start=False, stop=True).then_inc(s_pkv, 1)

            def attend(b):
                pe.wait_ge(s_q, b.times(2, 2))
                pe.wait_ge(s_m, b.times(1, 1))
                if b.i is not None or b.c >= 1:
                    pe.wait_ge(s_att, (b - 1).times(1, 1))
                for t in range(NT):
                    for c in range(KC):
                        mm = pe.matmul(ps_att[:, t, c * P:(c + 1) * P], q_t[:, c, t, :], kvm[:, c, :],
                                       start=True, stop=True)
                mm.then_inc(s_patt, 1)

            def transpose_h(b):
                pe.wait_ge(s_h, b.times(1, 1))
                if b.i is not None or b.c >= 1:
                    pe.wait_ge(s_ht, (b - 1).times(1, 1))
                for c in range(KC):
                    for t in range(NT):
                        mm = pe.transpose(ps_ht[:, c, t, :], h[:, b.buf(4), t, c * P:(c + 1) * P], ident[:])
                mm.then_inc(s_pht, 1)

            def multiply_ktv(b):
                pe.wait_ge(s_kv, b.times(1, 1))
                if b.i is not None or b.c >= 3:
                    pe.wait_ge(s_sc, (b - 3).times(1, 1))
                for c in range(KC):
                    mm = pe.matmul(ktv[:, c * P:(c + 1) * P], kv[:, 0, c * P:(c + 1) * P],
                                   kv[:, 1, c * P:(c + 1) * P], start=True, stop=True)
                mm.then_inc(s_pm, 1)

            def project_q(b, dc):
                if dc == 0:
                    if b.i is None and b.c == 0:
                        pe.wait_ge(s_w[2], 32)
                    pe.wait_ge(s_ht, b.times(1, 1))
                if b.i is not None or b.c >= 1:
                    pe.wait_ge(s_q, (b - 1).times(2, dc + 1))
                for c in range(KC):
                    mm = pe.matmul(ps_q[dc][:, 0:S], wq[:, c, dc * P:(dc + 1) * P], h_t[:, c, :, :],
                                   start=(c == 0), stop=(c == KC - 1))
                mm.then_inc(s_pq, 1)

            def transpose_h2(b):
                pe.wait_ge(s_h2, b.times(1, 1))
                if b.i is not None or b.c >= 1:
                    pe.wait_ge(s_h2t, (b - 1).times(1, 1))
                for c in range(KC):
                    for t in range(NT):
                        mm = pe.transpose(ps_h2t[:, c, t, :], rows[:, b.buf(4), t, c * P:(c + 1) * P], ident[:])
                mm.then_inc(s_ph2t, 1)

            def gate(b):
                pe.wait_ge(s_h2t, b.times(1, 1))
                pe.wait_ge(s_m, (b + 2).times(1, 1) if (b + 2).exists() else NB)
                if b.i is None and b.c >= NB - 2:
                    pe.wait_ge(s_sc, b.c)
                elif b.i is None and b.c == 0:
                    pe.wait_ge(s_w[3], 48)
                for t in range(NT):
                    for c in range(KC):
                        mm = pe.matmul(logits[:, t, :], h2_t[:, c, t, :], wg[:, c, :],
                                       start=(c == 0), stop=(c == KC - 1))
                mm.then_inc(s_pg, 1)

            def counted(t, weights, b, of):
                return pe.matmul(rank[:, t, :, :], weights[:], onehot[:, b.buf(2), of, :, :],
                                 start=False, stop=False, skip_group_check=True)

            def close_ranks(b):
                pe.wait_ge(s_pick, b.times(1, 1))
                counted(0, not_before, b, 0)
                counted(0, ones_bf, b, 1)
                return counted(1, not_before, b, 1)

            def rank_tokens(b):
                pe.wait_ge(s_oh, b.times(1, 1))
                if b.i is not None or b.c >= 1:
                    close_ranks(b - 1)
                counted(0, before, b, 0)
                counted(1, ones_bf, b, 0)
                counted(1, before, b, 1).then_inc(s_prk, 1)

            def step(s):
                if (s - 1).exists():
                    attend(s - 1)
                if s.exists():
                    transpose_h(s)
                    project_kv(s)
                    project_q(s, 0)
                if (s - 3).exists():
                    rank_tokens(s - 3)
                if (s - 2).exists():
                    transpose_h2(s - 2)
                if s.exists():
                    multiply_ktv(s)
                    project_q(s, 1)
                if (s - 2).exists():
                    gate(s - 2)

            dense_steps(pe, step, 0, NB + 3)
            close_ranks(Batch(None, NB - 1)).then_inc(s_end, 1)

            pe.wait_ge(s_found, 1)
            for q in range(2):
                for n in range(4):
                    mm = pe.matmul(ps_table[q][0:1, n * P:(n + 1) * P], found[:, q, n // 2, n % 2:n % 2 + 1],
                                   ident[:], start=True, stop=True)
            mm.then_inc(s_tt, 1)

            def transpose_rows(j, loaded):
                pe.wait_ge(s_in[j], loaded)
                for t in range(2):
                    for c in range(KC):
                        mm = pe.transpose(ps_rt[j % 2][:, t, c, :], row_in[:, 2 * j + t, c * P:(c + 1) * P],
                                          ident[:])
                mm.then_inc(s_prt, 1)

            pe.wait_ge(s_table, 2)
            offsets = load_values(nc, pe, "expert_at", lambda at: table[0:1, 1, at[0], bass.ds(at[1], V)],
                                  V, (E - 1) * D)

            def multiply(k, i):
                at = offsets((k, i * V))
                for j in range(PAIRS):
                    last = isinstance(i, int) and k == 1 and i == TRIPS - 1 and j == PAIRS - 1
                    if not last:
                        transpose_rows((j + 1) % PAIRS, i * 32 + 32 * (k * TRIPS + 1 + (j + 1) // PAIRS))
                    number = i * PAIRS + (k * TRIPS * PAIRS + j)
                    pe.wait_ge(s_rt, number + 1)
                    if not (isinstance(i, int) and k == 0 and i == 0 and j < 3):
                        pe.wait_ge(s_y, number - 2)
                    for t in range(2):
                        o = ps_y[j % 3][:, t, :]
                        for c in range(KC):
                            pe.matmul(o, row_t[:, j % 2, t, c, :], we[:, c, bass.ds(at[2 * j + t], D)],
                                      start=(c == 0), stop=False)
                        mm = pe.matmul(o, ones_bf[:], be_rows[:, bass.ds(at[2 * j + t], D)],
                                       start=False, stop=True)
                    mm.then_inc(s_py, 1)

            pe.wait_ge(s_we, 16 * WE_PIECES)
            pe.wait_ge(s_eb, 16)
            transpose_rows(0, 32)
            expert_bodies(pe, multiply, 0, peel_first=True)
            expert_bodies(pe, multiply, 1, peel_last=True)

        @block.scalar
        def _(act):
            act.add_instruction(mybir.InstLoadActFuncSet(name=nc.get_next_instruction_name(),
                                                         act_func_set_id=LOG_EXP_SET, ins=[], outs=[]))
            act.wait_ge(s_zero, 1)

            def inverse_root(n, b):
                act.wait_ge(s_mv[n], b.times(1, 1))
                act.activation(lnv[:, n, :], mv[:, n, b.buf(2), :, 1], ACT.Ln, bias=eps[:, 0:1]).then_inc(s_ln[n], 1)
                act.wait_ge(s_ln[n], b.times(1, 1))
                act.activation(rstd[:, n, b.buf(2), :], lnv[:, n, :], ACT.Exp, scale=-0.5).then_inc(s_rstd[n], 1)

            def copy_q(b, dc):
                act.wait_ge(s_pq, b.times(2, dc + 1))
                if dc == 0 and (b.i is not None or b.c >= 1):
                    act.wait_ge(s_patt, (b - 1).times(1, 1))
                if b.i is None and b.c == 0:
                    act.wait_ge(s_w[2], 32)
                act.activation(q_t[:, dc, :, :].rearrange("p t n -> p (t n)"), ps_q[dc][:, 0:S], ACT.Identity,
                               bias=bq_sb[:, dc:dc + 1]).then_inc(s_q, 1)

            def gate_exps(b):
                act.wait_ge(s_gap, b.times(1, 1))
                if b.i is not None or b.c >= 1:
                    act.wait_ge(s_w1, (b - 1).times(1, 1))
                for t in range(NT):
                    act.activation(exps[:, t, :], scores[:, t, :], ACT.Exp, bias=neg_max[:, t:t + 1],
                                   accum_out=sums[:, t:t + 1])
                act.activation(exp_gap[:], gap[:], ACT.Exp).then_inc(s_exp, 1)

            def normalise_h2(b):
                act.wait_ge(s_nmr[2], b.times(1, 1))
                if b.i is not None or b.c >= 4:
                    act.wait_ge(s_row[b.buf(4)], (b - 4).uses(4, 64))
                for t in range(NT):
                    a = act.activation(rows[:, b.buf(4), t, 0:D], x1[:, b.buf(2), t, :], ACT.Identity,
                                       bias=nmr[:, 2, t:t + 1], scale=rstd[:, 2, b.buf(2), t:t + 1])
                a.then_inc(s_h2, 1)

            def copy_kv(b):
                act.wait_ge(s_pkv, b.times(1, 1))
                if b.i is not None or b.c >= 1:
                    act.wait_ge(s_pm, (b - 1).times(1, 1))
                act.activation(kv[:].rearrange("p a d -> p (a d)"), ps_kv[0:SC, :], ACT.Copy).then_inc(s_kv, 1)

            def normalise_x(b):
                act.wait_ge(s_nmr[0], b.times(1, 1))
                if b.i is not None or b.c >= 4:
                    act.wait_ge(s_att, (b - 4).times(1, 1))
                    act.wait_ge(s_pht, (b - 4).times(1, 1))
                for t in range(NT):
                    a = act.activation(h[:, b.buf(4), t, :], x_sb[:, b.buf(4), t, :], ACT.Identity,
                                       bias=nmr[:, 0, t:t + 1], scale=rstd[:, 0, b.buf(2), t:t + 1])
                a.then_inc(s_h, 1)

            def copy_h_t(b):
                act.wait_ge(s_pht, b.times(1, 1))
                if b.i is not None or b.c >= 1:
                    act.wait_ge(s_pq, (b - 1).times(2, 2))
                act.activation(h_t[:], ps_ht[:], ACT.Copy).then_inc(s_ht, 1)

            def copy_h2_t(b):
                act.wait_ge(s_ph2t, b.times(1, 1))
                if b.i is not None or b.c >= 1:
                    act.wait_ge(s_pg, (b - 1).times(1, 1))
                act.activation(h2_t[:], ps_h2t[:], ACT.Copy).then_inc(s_h2t, 1)

            def step(s):
                p, b, f, nxt = s - 1, s - 2, s - 3, s + 1
                if b.exists():
                    inverse_root(2, b)
                if s.exists():
                    copy_h_t(s)
                if b.exists():
                    normalise_h2(b)
                if nxt.exists():
                    inverse_root(0, nxt)
                if s.exists():
                    copy_kv(s)
                if f.exists():
                    gate_exps(f)
                if p.exists():
                    inverse_root(1, p)
                if s.exists():
                    copy_q(s, 0)
                if b.exists():
                    copy_h2_t(b)
                if s.exists():
                    copy_q(s, 1)
                if nxt.exists():
                    normalise_x(nxt)

            dense_steps(act, step, -1, NB + 3)

            fill(act, 0, bin_ends(act, 0, E // 2, E))
            ends1 = bin_ends(act, 1, 0, E)

            def weigh(k, i):
                for j in range(PAIRS):
                    act.wait_ge(s_py, i * PAIRS + (k * TRIPS * PAIRS + j + 1))
                    if not (isinstance(i, int) and k == 0):
                        act.wait_ge(s_add[j], i * 32 + 32 * k * TRIPS)
                    if isinstance(i, int) and k == 0:
                        fill(act, 1, {e: ends1[e] for e in range(j, E, PAIRS)})
                    for t in range(2):
                        a = act.activation(y[:, 2 * j + t, :], ps_y[j % 3][:, t, :], ACT.Relu,
                                           scale=row_in[:, 2 * j + t, W_COL + k:W_COL + k + 1])
                    a.then_inc(s_y, 1)

            for k in range(2):
                expert_bodies(act, weigh, k, peel_first=(k == 0))

        @block.vector
        def _(dve):
            dve.memset(eps[:], EPS).then_inc(s_zero, 1)
            dve.memset(bkv_rows[:].bitcast(U32), 0).then_inc(s_zero, 1)

            def split(src, rest, part, n):
                dve.tensor_copy(part[:, 0, :], src).then_inc(s_split, 1)
                dve.wait_ge(s_split, n + 1)
                dve.tensor_tensor(rest[:, 0, :], src, part[:, 0, :], ALU.subtract).then_inc(s_split, 1)
                dve.wait_ge(s_split, n + 2)
                dve.tensor_copy(part[:, 1, :], rest[:, 0, :]).then_inc(s_split, 1)
                dve.wait_ge(s_split, n + 3)
                dve.tensor_tensor(rest[:, 1, :], rest[:, 0, :], part[:, 1, :], ALU.subtract).then_inc(s_split, 1)
                dve.wait_ge(s_split, n + 4)
                dve.tensor_copy(part[:, 2, :], rest[:, 1, :]).then_inc(s_split, 1)

            def stats(n, b, src):
                for t in range(NT):
                    i = dve.bn_stats(st[:, n, t, :], src[:, t, :])
                i.then_inc(s_st[n], 1)

            def moments(n, b):
                for t in range(NT):
                    i = dve.bn_aggr(mv[:, n, b.buf(2), t, :], st[:, n, t, :])
                i.then_inc(s_mv[n], 1)

            def mean_shift(n, b):
                dve.wait_ge(s_rstd[n], b.times(1, 1))
                dve.scalar_tensor_tensor(out=nmr[:, n, :], in0=mv[:, n, b.buf(2), :, 0], scalar=-1.0,
                                         in1=rstd[:, n, b.buf(2), :], op0=ALU.mult,
                                         op1=ALU.mult).then_inc(s_nmr[n], 1)

            def place(b):
                dve.wait_ge(s_sum, b.times(1, 1))
                if b.i is not None or b.c >= 2:
                    dve.wait_ge(s_row[(b - 2).buf(4)], (b - 2).uses(4, 64))
                dve.scalar_tensor_tensor(out=pos[:, b.buf(2)].rearrange("p t c -> p (t c)"),
                                         in0=signed_pos[:], scalar=-1.0, in1=signed_pos[:],
                                         op0=ALU.mult, op1=ALU.max).then_inc(s_pos, 1)

            def advance_ids(b):
                ids = rows[:, b.buf(4), :, ID_COL].bitcast(I32)
                if b.i is not None or b.c >= 4:
                    dve.wait_ge(s_row[b.buf(4)], (b - 4).uses(4, 64))
                    dve.tensor_scalar(ids, ids, 4 * S, None, ALU.add).then_inc(s_id, 1)
                else:
                    dve.sem_inc(s_id, 1)

            def copy_scores(b):
                dve.wait_ge(s_pg, b.times(1, 1))
                if b.i is not None or b.c >= 1:
                    dve.wait_ge(s_exp, (b - 1).times(1, 1))
                dve.tensor_copy(scores[:], logits).then_inc(s_sc, 1)

            def top_values(b):
                for t in range(NT):
                    i = dve.max(top[:, t, :], scores[:, t, :])
                i.then_inc(s_top, 1)

            def score_gaps(b):
                dve.wait_ge(s_top, b.times(1, 1))
                dve.tensor_scalar(neg_max[:], top[:, :, 0], -1.0, None, ALU.mult)
                dve.tensor_tensor(gap[:], top[:, :, 1], top[:, :, 0], ALU.subtract).then_inc(s_gap, 1)

            def top_indices(b):
                for t in range(NT):
                    i = dve.max_index(top_i[:, t, :], top[:, t, :], scores[:, t, :])
                i.then_inc(s_topi, 1)

            def indices_as_floats(b):
                dve.wait_ge(s_topi, b.times(1, 1))
                dve.tensor_copy(top_f[:], top_i[:, :, 0:2]).then_inc(s_topf, 1)

            def mark_experts(b):
                dve.wait_ge(s_topf, b.times(1, 1))
                dve.tensor_tensor(onehot[:, b.buf(2)].rearrange("p t c e -> p (t c) e"),
                                  iota_e[:].unsqueeze(1).to_broadcast([P, NT * 2, E]),
                                  top_f[:].rearrange("p t c -> p (t c)").unsqueeze(2)
                                  .to_broadcast([P, NT * 2, E]), ALU.is_equal).then_inc(s_oh, 1)

            def first_weights(b):
                dve.wait_ge(s_exp, b.times(1, 1))
                dve.reciprocal(rows[:, b.buf(4), :, W_COL], sums[:]).then_inc(s_w0, 1)

            def second_weights(b):
                dve.wait_ge(s_w0, b.times(1, 1))
                dve.tensor_tensor(rows[:, b.buf(4), :, W_COL + 1], rows[:, b.buf(4), :, W_COL], exp_gap[:],
                                  ALU.mult).then_inc(s_w1, 1)

            def pick_ranks(b):
                dve.wait_ge(s_prk, b.times(1, 1))
                dve.tensor_tensor(picked[:], rank.rearrange("p t c e -> p (t c) e"),
                                  onehot[:, b.buf(2)].rearrange("p t c e -> p (t c) e"),
                                  ALU.mult).then_inc(s_pick, 1)

            def sum_ranks(b):
                dve.wait_ge(s_pick, b.times(1, 1))
                dve.tensor_reduce(signed_pos[:], picked[:], AX_X, ALU.add).then_inc(s_sum, 1)

            def add_attention(b):
                dve.wait_ge(s_patt, b.times(1, 1))
                dve.wait_ge(s_h, b.times(1, 1))
                dve.tensor_tensor(att[:], ps_att[:], h[:, b.buf(4)], ALU.add).then_inc(s_att, 1)

            def mask_ktv(b):
                dve.wait_ge(s_pm, b.times(1, 1))
                if b.i is not None or b.c >= 1:
                    dve.wait_ge(s_patt, (b - 1).times(1, 1))
                dve.tensor_tensor(kvm[:].rearrange("p c n -> p (c n)"), ktv,
                                  head_mask[:].rearrange("p c n -> p (c n)"), ALU.mult).then_inc(s_m, 1)

            def scale(b):
                dve.wait_ge(s_mv[1], b.times(1, 1))
                for t in range(NT):
                    i = dve.scalar_tensor_tensor(out=scaled[:, t, :], in0=att[:, t, :],
                                                 scalar=mv[:, 1, b.buf(2), t, 0:1], in1=gamma_sb[:],
                                                 op0=ALU.subtract, op1=ALU.mult)
                i.then_inc(s_scaled, 1)

            def finish_x1(b):
                dve.wait_ge(s_scaled, b.times(1, 1))
                dve.wait_ge(s_rstd[1], b.times(1, 1))
                dve.wait_ge(s_xb, b.times(1, 1))
                if b.i is not None or b.c >= 2:
                    dve.wait_ge(s_h2, (b - 2).times(1, 1))
                    dve.wait_ge(s_x1w[b.buf(2)], (b - 2).uses(2, 16))
                for t in range(NT):
                    i = dve.scalar_tensor_tensor(out=x1[:, b.buf(2), t, :], in0=scaled[:, t, :],
                                                 scalar=rstd[:, 1, b.buf(2), t:t + 1],
                                                 in1=x_beta[:, b.buf(2), t, :], op0=ALU.mult, op1=ALU.add)
                i.then_inc(s_x1, 1)

            def step(s):
                p, b, f, g, nxt = s - 1, s - 2, s - 3, s - 4, s + 1
                if s.i is None and s.c == 0:
                    dve.memset(zeros[:], 0.0).then_inc(s_zero, 1)
                    dve.wait_ge(s_const, 1)
                if s.i is None and s.c == 1:
                    dve.memset(be_rows[:].bitcast(U32), 0).then_inc(s_zero, 1)
                    dve.wait_ge(s_be_in, 16)
                    split(be_in[:], be_rest, be_part, 5)
                    dve.wait_ge(s_w[3], 48)
                if b.exists():
                    dve.wait_ge(s_x1, b.times(1, 1))
                    stats(2, b, x1[:, b.buf(2)])
                if f.exists():
                    copy_scores(f)
                if g.exists():
                    place(g)
                if f.exists():
                    advance_ids(f)
                    dve.wait_ge(s_sc, f.times(1, 1))
                if b.exists():
                    dve.wait_ge(s_st[2], b.times(1, 1))
                if b.exists() or f.exists():
                    settle(dve, s_passed[0])
                if b.exists():
                    moments(2, b)
                if f.exists():
                    top_values(f)
                if nxt.exists():
                    dve.wait_ge(s_x[nxt.buf(4)], nxt.uses(4, 16))
                    if nxt.i is not None or nxt.c >= 1:
                        dve.wait_ge(s_mv[0], (nxt - 1).times(1, 1))
                    stats(0, nxt, x_sb[:, nxt.buf(4)])
                if b.exists():
                    mean_shift(2, b)
                if f.exists():
                    score_gaps(f)
                if nxt.exists():
                    dve.wait_ge(s_st[0], nxt.times(1, 1))
                if nxt.exists() or f.exists():
                    settle(dve, s_passed[0])
                if f.exists():
                    top_indices(f)
                if nxt.exists():
                    moments(0, nxt)
                if f.exists():
                    indices_as_floats(f)
                if p.exists():
                    add_attention(p)
                if f.exists():
                    mark_experts(f)
                if p.exists():
                    dve.wait_ge(s_att, p.times(1, 1))
                    stats(1, p, att)
                if nxt.exists():
                    mean_shift(0, nxt)
                if p.exists():
                    dve.wait_ge(s_st[1], p.times(1, 1))
                    settle(dve, s_passed[0])
                    moments(1, p)
                if f.exists():
                    pick_ranks(f)
                if p.exists():
                    scale(p)
                if s.exists():
                    mask_ktv(s)
                if f.exists():
                    first_weights(f)
                    sum_ranks(f)
                if p.exists():
                    finish_x1(p)
                if f.exists():
                    second_weights(f)

            dve.wait_ge(s_w[1], 16)
            split(bkv_in[:], bkv_rest, bkv_part, 0)
            dense_steps(dve, step, -1, NB + 4)

            steps = [0]

            def done(*ins):
                steps[0] += 1
                ins[-1].then_inc(s_tab, 1)
                dve.wait_ge(s_tab, steps[0])

            base0 = bin_base[:, 0]
            dve.wait_ge(s_end, 1)
            done(dve.tensor_copy(ends[:], rank[:, 0]))
            pairs = ends[:].rearrange("p c (r o) -> p c r o", o=2)
            pad_pairs = pad_at[:].rearrange("p c (r o) -> p c r o", o=2)
            dve.tensor_copy(pad_pairs[:, :, :, 0], pairs[:, :, :, 0])
            dve.tensor_scalar(pad_pairs[:, :, :, 1], pairs[:, :, :, 1], -1.0, float(1 - P), ALU.mult,
                              ALU.add).then_inc(s_pad, 1)
            done(dve.tensor_tensor(counts[:], ends[:], base0, ALU.subtract))
            done(dve.tensor_scalar(cnt_i[:], counts[:], float(P - 1), None, ALU.add))
            done(dve.tensor_scalar(tiles_i[:], cnt_i[:], P.bit_length() - 1, None, ALU.logical_shift_right))
            done(dve.tensor_copy(tiles_f[:], tiles_i[:]), dve.tensor_copy(scan[:, 0], tiles_i[:]))
            sh = shift[:, :, 0:E].rearrange("p c (r o) -> p c r o", o=2)
            bp = base0.rearrange("p c (r o) -> p c r o", o=2)
            tp = tiles_f[:].rearrange("p c (r o) -> p c r o", o=2)
            dve.tensor_copy(sh[:, :, :, 0], bp[:, :, :, 0])
            for k in range(2):
                dve.scalar_tensor_tensor(out=sh[:, k, :, 1], in0=tp[:, k, :, 1], scalar=float(P),
                                         in1=bp[:, k, :, 1], op0=ALU.mult, op1=ALU.add)
            a, d = 0, 1
            while d < E:
                done(dve.tensor_copy(scan[:, 1 - a, :, 0:d], scan[:, a, :, 0:d]),
                     dve.tensor_tensor(scan[:, 1 - a, :, d:E], scan[:, a, :, d:E], scan[:, a, :, 0:E - d],
                                       ALU.add))
                a, d = 1 - a, 2 * d
            upto, before_e = scan[:, a], scan[:, 1 - a]
            done(dve.tensor_scalar(sh[:, :, :, 1], sh[:, :, :, 1], -1.0, 1.0, ALU.mult, ALU.add),
                 dve.tensor_scalar(shift[:, :, E], upto[:, :, E - 1], -float(P), float(SPARE), ALU.mult, ALU.add),
                 dve.tensor_tensor(before_e, upto, tiles_f[:], ALU.subtract))
            done(dve.scalar_tensor_tensor(out=shift[:, :, 0:E], in0=before_e, scalar=-float(P),
                                          in1=shift[:, :, 0:E], op0=ALU.mult, op1=ALU.add),
                 dve.tensor_tensor(reached[:], tile_no[:].unsqueeze(1).unsqueeze(3).to_broadcast([P, 2, 2, E]),
                                   upto.unsqueeze(2).to_broadcast([P, 2, 2, E]), ALU.is_ge))
            done(dve.tensor_tensor(delta[:], shift[:, :, 1:E + 1], shift[:, :, 0:E], ALU.subtract),
                 dve.tensor_reduce(found[:, 1], reached[:], AX_X, ALU.add))
            done(dve.tensor_tensor(reached_d[:], reached[:],
                                   delta[:].unsqueeze(2).to_broadcast([P, 2, 2, E]), ALU.mult))
            done(dve.tensor_reduce(found[:, 0], reached_d[:], AX_X, ALU.add))
            done(dve.tensor_tensor(found[:, 0], found[:, 0],
                                   shift[:, :, 0:1].to_broadcast([P, 2, 2]), ALU.add))
            dve.scalar_tensor_tensor(out=found[:, 0], in0=tile_no[:].unsqueeze(1).to_broadcast([P, 2, 2]),
                                     scalar=float(P), in1=found[:, 0], op0=ALU.mult, op1=ALU.add)
            dve.tensor_scalar(found[:, 1], found[:, 1], float(E - 1), float(D), ALU.min,
                              ALU.mult).then_inc(s_found, 1)
            dve.wait_ge(s_tt, 1)
            for q in range(2):
                dve.tensor_copy(table[:, q].rearrange("o c t -> o (c t)"),
                                ps_table[q][0:1, 0:4 * P]).then_inc(s_table, 1)

            def copy_rows(k, i):
                for j in range(PAIRS):
                    number = i * PAIRS + (k * TRIPS * PAIRS + j)
                    dve.wait_ge(s_prt, number + 1)
                    if not (isinstance(i, int) and k == 0 and j < 2):
                        dve.wait_ge(s_py, number - 1)
                    dve.tensor_copy(row_t[:, j % 2], ps_rt[j % 2][:]).then_inc(s_rt, 1)

            for k in range(2):
                expert_bodies(dve, copy_rows, k, peel_first=(k == 0))


def kernel(**inputs):
    import numpy as np
    import concourse.bacc as bacc
    from concourse.bass_utils import run_bass_kernel_spmd

    g = {n.replace("L0_xattn_", "").replace("L0_ffn_", ""): np.asarray(v) for n, v in inputs.items()}
    c = np.ascontiguousarray
    arrays = {
        "x": c(g["x"].reshape(TOK, D)),
        "ctx_t": c(g["ctx_1024"].transpose(0, 2, 1).reshape(NB, KC, P, SC).transpose(0, 2, 1, 3)),
        "wkv_t": c(np.concatenate([g["Wk"].T, g["Wv"].T], axis=1)),
        "wq_t": c(g["Wq"].T),
        "gate_t": c(g["gate_w"].T),
        "we_t": c(g["expert_w"].transpose(2, 0, 1).reshape(D, E * D)),
        "bkv": c(np.concatenate([g["bk"], g["bv"]])),
        "be": c(g["expert_b"].reshape(E * D)),
        "bq": c(g["bq"].reshape(KC, P).T),
        "gamma": c(g["ln_gamma"]),
        "beta": c(g["ln_beta"]),
    }
    nc = bacc.Bacc("TRN2", target_bir_lowering=False, num_devices=1)
    args = [nc.dram_tensor(f"in_{n}", a.shape, mybir.dt.from_np(a.dtype), kind="ExternalInput").ap()
            for n, a in arrays.items()]
    out = nc.dram_tensor("out_rows", (OUT_ROWS, D), F32, kind="ExternalOutput").ap()
    build(nc, *args, out)
    r = run_bass_kernel_spmd(nc, [{f"in_{n}": a for n, a in arrays.items()}], core_ids=[0])
    return r.results[0]["out_rows"][0:TOK].reshape(NB, S, D)
```

```python
from contextlib import ExitStack

import concourse.bass as bass
from concourse import mybir

F32 = mybir.dt.float32
F32R = mybir.dt.float32r
BF16 = mybir.dt.bfloat16
I32 = mybir.dt.int32
U32 = mybir.dt.uint32
ALU = mybir.AluOpType
ACT = mybir.ActivationFunctionType
AX_X = mybir.AxisListType.X

P = 128
NB, S, D = 64, 256, 256
SC = 120
NH = 16
E = 16
NT = S // P
KC = D // P
TOK = NB * S
SCALE = (D // NH) ** -0.5
EPS = 1e-5

ROW = D + 4
W_COL, ID_COL = D, D + 2
PAD = P
REGION = TOK + 2 * PAD
TILES = TOK // P + E
SPARE = E // 2 * REGION
ROWS = SPARE + E * P
PAD_ID = TOK
OUT_ROWS = TOK + 2 * E * P

U = 8
LEAD, LOOPS = 12, (NB - 4 - 12) // U
V = 16
PAIRS = V // 2
TRIPS = TILES // V
WE_PIECES = 8
TAILS = 2 * E // 4
LOG_EXP_SET = 6


class Batch:

    def __init__(self, i, c):
        self.i, self.c = i, c

    def __sub__(self, n):
        return Batch(self.i, self.c - n)

    def __add__(self, n):
        return Batch(self.i, self.c + n)

    def exists(self, low=0):
        return self.i is not None or low <= self.c < NB

    def times(self, k, plus=0):
        n = k * self.c + plus
        return n if self.i is None else self.i * (k * U) + n

    def uses(self, bufs, k):
        n = k * (self.c // bufs + 1)
        return n if self.i is None else self.i * (k * U // bufs) + n

    def buf(self, bufs):
        return self.c % bufs


def settle(eng, passed):
    eng.sem_inc(passed, 1)


def dense_steps(eng, step, low, high):
    for s in range(low, LEAD):
        step(Batch(None, s))
    with eng.Fori(0, LOOPS) as i:
        for j in range(U):
            step(Batch(i, LEAD + j))
    for s in range(LEAD + LOOPS * U, high):
        step(Batch(None, s))


def expert_bodies(eng, body, k, peel_first=False, peel_last=False):
    if peel_first:
        body(k, 0)
    with eng.Fori(int(peel_first), TRIPS - int(peel_last)) as i:
        body(k, i)
    if peel_last:
        body(k, TRIPS - 1)


def table_reader(nc, eng, table, column, max_val):
    regs = [eng.alloc_register(f"column{column}_{n}") for n in range(V)]

    def read(k, i):
        half = int(isinstance(i, int) and i * V >= P)
        row = (column * 2 + k) * 2 + half
        eng.load(regs, table[row:row + 1, bass.ds(i * V - half * P, V)])
        return [nc.snap(r, min_val=0, max_val=max_val) for r in regs]

    return read


def build(nc, x, ctx_t, wkv_t, wq_t, gate_t, we_t, bkv, be, bq, gamma, beta, out):
    bins = [nc.dram_tensor(f"bins{k}", [ROWS, ROW], F32, kind="Internal").ap() for k in range(2)]
    bkv_dram = nc.dram_tensor("bkv_dram", [3, 2 * D], BF16, kind="Internal").ap()
    be_dram = nc.dram_tensor("be_dram", [3, E * D], BF16, kind="Internal").ap()

    def parts_as_rows(dram):
        return dram.rearrange("n (p m) -> p n m", p=P)

    with ExitStack() as ctx:
        def sb(name, shape, dt=F32):
            return ctx.enter_context(nc.sbuf_tensor(name, shape, dt))

        def ps(name, shape, dt=F32):
            return ctx.enter_context(nc.psum_tensor(name, shape, dt))

        def sem(name):
            return ctx.enter_context(nc.semaphore(name))

        ident = sb("ident", [P, P])
        ones_row = sb("ones_row", [1, P])
        ones_bf = sb("ones_bf", [P, P], BF16)
        before = sb("before", [P, P], BF16)
        not_before = sb("not_before", [P, P], BF16)
        head_mask = sb("head_mask", [P, KC, P])
        iota_e = sb("iota_e", [P, E])
        id_step = sb("id_step", [P, NT], I32)
        tile_no = sb("tile_no", [P, 2])
        bin_base = sb("bin_base", [P, NT, 2, E])
        eps = sb("eps", [P, 1])
        wkv_head = sb("wkv_head", [P, KC, 2 * D], F32R)
        wkv_rest = sb("wkv_rest", [P, KC, 2 * D], F32R)
        wq = sb("wq", [P, KC, D])
        wg = sb("wg", [P, KC, E])
        we = sb("we", [P, KC, E * D])
        we_head = sb("we_head", [P, KC, E * D], F32R)
        we_rest = we[:].bitcast(F32R)
        bkv_rows = sb("bkv_rows", [P, 2 * D], BF16)
        be_rows = sb("be_rows", [P, E * D], BF16)
        bkv_in = sb("bkv_in", [P, 2 * D // P])
        be_in = sb("be_in", [P, E * D // P])
        bkv_rest = sb("bkv_rest", [P, 2, 2 * D // P])
        be_rest = sb("be_rest", [P, 2, E * D // P])
        bkv_part = sb("bkv_part", [P, 3, 2 * D // P], BF16)
        be_part = sb("be_part", [P, 3, E * D // P], BF16)
        bq_sb = sb("bq_sb", [P, KC])
        gamma_sb = sb("gamma_sb", [P, D])
        beta_sb = sb("beta_sb", [P, D])
        pad_rows = sb("pad_rows", [P, E, ROW])
        spare_rows = sb("spare_rows", [P, E, ROW])

        xh = sb("xh", [P, 2, 4 * NT, D])
        x_sb, h = [xh[:, n].rearrange("p (b t) d -> p b t d", t=NT) for n in range(2)]
        c_sb = sb("c_sb", [P, 4, KC, SC])
        c_head = sb("c_head", [P, 2, KC, SC], F32R)
        c_rest = sb("c_rest", [P, 2, KC, SC], F32R)
        h_t = sb("h_t", [P, KC, NT, P])
        kv = sb("kv", [SC, 2, D])
        q_t = sb("q_t", [P, KC, NT, P])
        kvm = sb("kvm", [P, KC, P])
        att = sb("att", [P, NT, D])
        scaled = sb("scaled", [P, NT, D])
        x_beta = sb("x_beta", [P, 2, NT, D])
        x1 = sb("x1", [P, 2, NT, D])
        rows = sb("rows", [P, 4, NT, ROW])
        h2_t = sb("h2_t", [P, KC, NT, P])
        st = sb("st", [P, 3, NT, 6])
        mv = sb("mv", [P, 3, 2, NT, 2])
        lnv = sb("lnv", [P, 3, NT])
        rstd = sb("rstd", [P, 3, 2, NT])
        nmr = sb("nmr", [P, 3, NT])
        scores = sb("scores", [P, NT, E])
        top = sb("top", [P, NT, 8])
        top_i = sb("top_i", [P, NT, 8], U32)
        top_f = sb("top_f", [P, NT, 2])
        neg_max = sb("neg_max", [P, NT])
        gap = sb("gap", [P, NT])
        exps = sb("exps", [P, NT, E])
        sums = sb("sums", [P, NT])
        exp_gap = sb("exp_gap", [P, NT])
        onehot = sb("onehot", [P, 2, NT, 2, E], BF16)
        picked = sb("picked", [P, NT * 2, E])
        signed_pos = sb("signed_pos", [P, NT * 2])
        pos = sb("pos", [P, 2, NT, 2], I32)

        ends = sb("ends", [P, 2, E])
        counts = sb("counts", [P, 2, E])
        pad_at = sb("pad_at", [P, 2, E], I32)
        cnt_i = sb("cnt_i", [P, 2, E], I32)
        tiles_i = sb("tiles_i", [P, 2, E], I32)
        tiles_f = sb("tiles_f", [P, 2, E])
        scan = sb("scan", [P, 2, 2, E])
        shift = sb("shift", [P, 2, E + 1])
        delta = sb("delta", [P, 2, E])
        reached = sb("reached", [P, 2, 2, E])
        reached_d = sb("reached_d", [P, 2, 2, E])
        found = sb("found", [P, 2, 2, 2])
        table = sb("table", [8, P], I32)

        row_in = sb("row_in", [P, V, ROW])
        zeros = row_in[:].rearrange("p v r -> p (v r)")[:, 0:4 * D]
        wkv = row_in[:].rearrange("p v r -> p (v r)")[:, 4 * D:8 * D].rearrange("p (c n) -> p c n", c=KC)
        row_head = sb("row_head", [P, 2, 2, KC, P], F32R)
        row_rest = sb("row_rest", [P, 2, 2, KC, P], F32R)
        y = xh[:].rearrange("p a t d -> p (a t) d")[:, 0:V]

        ps_ht = ps("ps_ht", [P, KC, NT, P])
        ps_kv = ps("ps_kv", [P, 2 * D])
        ps_q = [ps(f"ps_q{n}", [P, 512]) for n in range(KC)]
        ps_mg = ps("ps_mg", [P, 512])
        ps_att = ps("ps_att", [P, NT, D])
        ps_h2t = ps("ps_h2t", [P, KC, NT, P])
        ps_rank = ps("ps_rank", [P, 512])
        ktv = ps_mg[:, 0:D]
        logits = ps_mg[:, D:D + NT * E].rearrange("p (t e) -> p t e", e=E)
        rank = ps_rank[:, 0:NT * 2 * E].rearrange("p (t c e) -> p t c e", t=NT, e=E)
        ps_rt = [ps_ht, ps_h2t]
        ps_y = [ps_att] + [b[:].rearrange("p (t d) -> p t d", t=2) for b in (ps_q[1], ps_kv, ps_q[0])]
        YB = len(ps_y)

        s_w = [sem(f"weights{n}_loaded") for n in range(4)]
        s_we = [sem(f"expert_weights_loaded{n}") for n in range(WE_PIECES)]
        s_whead = sem("weight_heads_ready")
        s_wrest = sem("weight_rests_ready")
        s_be_in = sem("expert_bias_loaded")
        s_const = sem("pool_constants_made")
        s_step = sem("pool_step_done")
        s_passed = [sem(f"passed_by_{n}") for n in ("dve", "pool")]
        s_zero = sem("zeros_made")
        s_split = sem("bias_split_step")
        s_kvb = sem("kv_bias_rows_placed")
        s_eb = sem("expert_bias_rows_placed")
        s_kvd = sem("kv_bias_parts_in_dram")
        s_ebd = sem("expert_bias_parts_in_dram")
        s_init = sem("dram_fill_written")
        s_rank0 = sem("rank_started")
        s_x = [sem(f"x_loaded{n}") for n in range(4)]
        s_c = [sem(f"context_loaded{n}") for n in range(4)]
        s_wkvh = sem("kv_weight_heads_ready")
        s_wkvr = sem("kv_weight_rests_ready")
        s_chead = sem("context_head_ready")
        s_crest = sem("context_rest_ready")
        s_x1w = [sem(f"x1_written{n}") for n in range(2)]
        s_row = [sem(f"rows_scattered{n}") for n in range(4)]
        s_st = [sem(f"stats{n}_ready") for n in range(3)]
        s_mv = [sem(f"moments{n}_ready") for n in range(3)]
        s_ln = [sem(f"log_var{n}_ready") for n in range(3)]
        s_rstd = [sem(f"rstd{n}_ready") for n in range(3)]
        s_nmr = {0: sem("shift0_ready"), 2: sem("shift2_ready")}
        s_h = sem("h_ready")
        s_pht = sem("h_transposed")
        s_ht = sem("h_t_copied")
        s_pkv = sem("kv_projected")
        s_kv = sem("kv_copied")
        s_pq = sem("q_projected")
        s_q = sem("q_copied")
        s_pm = sem("ktv_multiplied")
        s_m = sem("ktv_masked")
        s_patt = sem("attention_multiplied")
        s_att = sem("attention_residual_ready")
        s_scaled = sem("scaled_ready")
        s_xb = sem("x_beta_ready")
        s_x1 = sem("x1_tile_ready")
        s_h2 = sem("h2_ready")
        s_ph2t = sem("h2_transposed")
        s_h2t = sem("h2_t_copied")
        s_pg = sem("logits_ready")
        s_sc = sem("scores_copied")
        s_top = sem("top_values_ready")
        s_topi = sem("top_indices_ready")
        s_gap = sem("gap_ready")
        s_topf = sem("indices_as_floats")
        s_oh = sem("onehot_ready")
        s_exp = sem("exps_ready")
        s_w0 = sem("first_weight_ready")
        s_w1 = sem("second_weight_ready")
        s_id = sem("ids_advanced")
        s_prk = sem("ranks_ready")
        s_pick = sem("rank_picked")
        s_sum = sem("signed_position_ready")
        s_pos = sem("positions_ready")
        s_end = sem("rank_ends_ready")
        s_pad = sem("pad_positions_ready")
        s_padw = [sem(f"pad_rows_written{k}") for k in range(2)]
        s_tab = sem("table_step")
        s_found = sem("table_columns_ready")
        s_tt = sem("table_transposed")
        s_table = sem("table_placed")
        s_in = [sem(f"row_pair_loaded{n}") for n in range(PAIRS)]
        s_prt = sem("row_pair_transposed")
        s_rhead = sem("row_heads_ready")
        s_rt = sem("row_pair_copied")
        s_py = sem("pair_multiplied")
        s_y = sem("pair_result_ready")
        s_add = [sem(f"pair_result_added{n}") for n in range(PAIRS)]

        x_v = x.rearrange("(n p t) d -> n p t d", p=P, t=NT)
        out_v = out[0:TOK, :].rearrange("(n p t) d -> n p t d", p=P, t=NT)

        def batch_of(view, b):
            if b.i is None:
                return view[b.c]
            return view[bass.ds(b.times(1), 1)].rearrange("o p a d -> (o p) a d")

        def pieces(step, each):
            return range(min(step * each, WE_PIECES), min((step + 1) * each, WE_PIECES))

        def piece(n):
            return slice(n * E * D // WE_PIECES, (n + 1) * E * D // WE_PIECES)

        def fill(eng, k, low, high):
            eng.wait_ge(s_pad, 1)
            regs = [eng.alloc_register(f"pad{k}_{e}") for e in range(low, high)]
            eng.load(regs, pad_at[0:1, k, low:high])
            for e, reg in zip(range(low, high), regs):
                at = nc.snap(reg, min_val=0, max_val=SPARE - P)
                eng.dma_start(bins[k][bass.ds(at, P), :], pad_rows[:, e, :]).then_inc(s_padw[k], 16)
            for reg in regs:
                eng.free_register(reg)

        block = ctx.enter_context(nc.Block())

        @block.sync
        def _(sp):
            def load(b):
                n = b.buf(4)
                if b.i is not None or b.c >= 4:
                    sp.wait_ge(s_xb, (b - 4).times(1, 1))
                    sp.wait_ge(s_h, (b - 4).times(1, 1))
                    sp.wait_ge(s_crest, (b - 4).times(1, 1))
                sp.dma_start(x_sb[:, n], batch_of(x_v, b)).then_inc(s_x[n], 16)
                sp.dma_start(c_sb[:, n], batch_of(ctx_t, b)).then_inc(s_c[n], 16)

            load(Batch(None, 0))
            sp.dma_start(bkv_in[:], bkv.rearrange("(p n) -> p n", p=P)).then_inc(s_w[1], 16)
            sp.dma_start(wkv, wkv_t.rearrange("(c p) n -> p c n", p=P)).then_inc(s_w[0], 16)
            sp.dma_start(wq[:], wq_t.rearrange("(c p) n -> p c n", p=P)).then_inc(s_w[2], 16)
            sp.dma_start(bq_sb[:], bq).then_inc(s_w[2], 16)
            sp.dma_start(beta_sb[:], beta.partition_broadcast(P)).then_inc(s_w[3], 16)
            sp.dma_start(gamma_sb[:], gamma.partition_broadcast(P)).then_inc(s_w[3], 16)
            sp.dma_start(wg[:], gate_t.rearrange("(c p) n -> p c n", p=P)).then_inc(s_w[3], 16)
            load(Batch(None, 1))
            sp.wait_ge(s_split, 5)
            sp.dma_start(parts_as_rows(bkv_dram), bkv_part[:]).then_inc(s_kvd, 16)
            load(Batch(None, 2))
            sp.wait_ge(s_kvd, 16)
            sp.wait_ge(s_zero, 2)
            sp.dma_start(bkv_rows[0:65:32, :], bkv_dram).then_inc(s_kvb, 16)
            load(Batch(None, 3))
            sp.dma_start(be_in[:], be.rearrange("(p n) -> p n", p=P)).then_inc(s_be_in, 16)

            def prepare_experts(step):
                if step == 2:
                    sp.wait_ge(s_split, 10)
                    sp.dma_start(parts_as_rows(be_dram), be_part[:]).then_inc(s_ebd, 16)
                if step == 3:
                    sp.wait_ge(s_zero, 4)
                    sp.wait_ge(s_ebd, 16)
                    sp.dma_start(be_rows[0:65:32, :], be_dram).then_inc(s_eb, 16)
                if step < TAILS:
                    sp.wait_ge(s_zero, 3)
                    tail = out[TOK:OUT_ROWS, :].rearrange("(n p a) d -> n p (a d)", p=P, a=4)
                    sp.dma_start(tail[step], zeros).then_inc(s_init, 16)
                for n in pieces(step, 4):
                    sp.dma_start(we[:, :, piece(n)],
                                 we_t.rearrange("(c p) n -> p c n", p=P)[:, :, piece(n)]
                                 ).then_inc(s_we[n], 16)
                if step >= LEAD - 8:
                    q, k = divmod(step - (LEAD - 8), 2)
                    sp.wait_ge(s_const, 2)
                    sp.dma_start(bins[k][SPARE + 4 * q * P:SPARE + 4 * (q + 1) * P, :]
                                 .rearrange("(j p) d -> p j d", p=P),
                                 spare_rows[:, 4 * q:4 * q + 4, :]).then_inc(s_init, 16)

            def step(s):
                p = s - 1
                if p.exists():
                    sp.wait_ge(s_x1, p.times(NT, NT))
                    sp.dma_start(batch_of(out_v, p), x1[:, p.buf(2)]).then_inc(s_x1w[p.buf(2)], 16)
                nxt = s + 4
                if nxt.exists():
                    load(nxt)
                if s.i is None and s.c < LEAD:
                    prepare_experts(s.c)

            dense_steps(sp, step, 0, NB + 1)

            fill(sp, 0, 0, E // 2)
            for n in range(4):
                sp.wait_ge(s_row[n], 64 * (NB // 4))
            sp.wait_ge(s_init, 16 * (TAILS + 8))
            sp.wait_ge(s_table, 1)
            first_rows = table_reader(nc, sp, table, 0, ROWS - P)

            def load_rows(k, i):
                firsts = first_rows(k, i)
                if isinstance(i, int) and i == 0:
                    sp.wait_ge(s_padw[k], E * 16)
                for j in range(PAIRS):
                    if not (isinstance(i, int) and i == 0 and k == 0):
                        sp.wait_ge(s_add[j], i * 32 + 32 * k * TRIPS)
                    for t in range(2):
                        sp.dma_start(row_in[:, 2 * j + t, :],
                                     bins[k][bass.ds(firsts[2 * j + t], P), :]).then_inc(s_in[j], 16)
                if isinstance(i, int) and i == 0 and k == 0:
                    fill(sp, 1, 0, E // 2)
                    fill(sp, 1, E // 2, E)

            expert_bodies(sp, load_rows, 0, peel_first=True, peel_last=True)
            expert_bodies(sp, load_rows, 1, peel_first=True, peel_last=True)
            for j in range(PAIRS):
                sp.wait_ge(s_add[j], 2 * 32 * TRIPS)
            for n in range(2):
                sp.wait_ge(s_x1w[n], 16 * (NB // 2))

        @block.gpsimd
        def _(pool):
            steps = [0]

            def done(ins):
                steps[0] += 1
                ins.then_inc(s_step, 1)
                pool.wait_ge(s_step, steps[0])

            done(pool.memset(ident[:], 0.0))
            done(pool.affine_select(out=ident[:], in_=ident[:], compare_op=ALU.not_equal, fill=1.0, base=0,
                                    pattern=[[-1, P]], channel_multiplier=1))
            done(pool.memset(ones_bf[:], 1.0))
            done(pool.memset(ones_row[:], 1.0))
            done(pool.affine_select(out=before[:], in_=ones_bf[:], compare_op=ALU.is_gt, fill=0.0, base=0,
                                    pattern=[[1, P]], channel_multiplier=-1))
            done(pool.affine_select(out=not_before[:], in_=ones_bf[:], compare_op=ALU.is_ge, fill=0.0, base=0,
                                    pattern=[[-1, P]], channel_multiplier=1))
            G = D // NH
            mask = head_mask[:].rearrange("p c (g j) -> p c g j", j=G)
            done(pool.memset(head_mask[:], SCALE))
            done(pool.affine_select(out=mask, in_=mask, compare_op=ALU.is_ge, fill=0.0, base=0,
                                    pattern=[[0, KC], [-G, P // G], [0, G]], channel_multiplier=1))
            done(pool.affine_select(out=mask, in_=mask, compare_op=ALU.is_ge, fill=0.0, base=G - 1,
                                    pattern=[[0, KC], [G, P // G], [0, G]], channel_multiplier=-1))
            done(pool.iota(iota_e[:], [[1, E]], base=0, channel_multiplier=0,
                           allow_small_or_imprecise_dtypes=True))
            done(pool.iota(tile_no[:], [[P, 2]], base=0, channel_multiplier=1,
                           allow_small_or_imprecise_dtypes=True))
            base = bin_base[:].rearrange("p t c (r o) -> p (t c) r o", o=2)
            done(pool.iota(base[:, :, :, 0], [[0, NT * 2], [REGION, E // 2]], base=0, channel_multiplier=0,
                           allow_small_or_imprecise_dtypes=True))
            done(pool.iota(base[:, :, :, 1], [[0, NT * 2], [-REGION, E // 2]], base=1 - REGION,
                           channel_multiplier=0, allow_small_or_imprecise_dtypes=True))
            done(pool.iota(id_step[:], [[0, NT]], base=4 * S, channel_multiplier=0))
            done(pool.memset(rows[:, :, :, D:ROW], 0.0))
            ids = rows[:].bitcast(I32)[:, :, :, ID_COL]
            pool.iota(ids, [[S, 4], [1, NT]], base=0, channel_multiplier=NT).then_inc(s_const, 1)
            pool.wait_ge(s_w[3], 48)

            def make_pads():
                steps[0] += 1
                pool.wait_ge(s_const, 1)
                pool.memset(pad_rows[:], 0.0)
                pool.memset(spare_rows[:], 0.0).then_inc(s_step, 1)
                pool.wait_ge(s_step, steps[0])
                pool.iota(pad_rows[:].bitcast(I32)[:, :, ID_COL], [[P, E]], base=PAD_ID, channel_multiplier=1)
                pool.iota(spare_rows[:].bitcast(I32)[:, :, ID_COL], [[P, E]], base=PAD_ID + E * P,
                          channel_multiplier=1).then_inc(s_const, 1)

            def context_rest(b):
                pool.wait_ge(s_chead, b.times(1, 1))
                if b.i is not None or b.c >= 2:
                    pool.wait_ge(s_pkv, (b - 2).times(1, 1))
                pool.tensor_tensor(c_rest[:, b.buf(2)], c_sb[:, b.buf(4)],
                                   c_head[:, b.buf(2)].bitcast(F32),
                                   ALU.subtract).then_inc(s_crest, 1)

            context_rest(Batch(None, 0))

            def step(s):
                if (s + 1).exists():
                    context_rest(s + 1)
                if s.exists():
                    n = s.buf(2)
                    pool.wait_ge(s_x[s.buf(4)], s.uses(4, 16))
                    if s.i is not None or s.c >= 2:
                        pool.wait_ge(s_x1, (s - 2).times(NT, NT))
                    pool.tensor_tensor(x_beta[:, n], x_sb[:, s.buf(4)],
                                       beta_sb[:].unsqueeze(1).to_broadcast([P, NT, D]),
                                       ALU.add).then_inc(s_xb, 1)
                if s.i is None and s.c == 0:
                    make_pads()
                if s.i is None and s.c >= 1:
                    for n in pieces(s.c - 1, 2):
                        pool.wait_ge(s_whead, n + 1)
                        pool.tensor_tensor(we_rest[:, :, piece(n)], we[:, :, piece(n)],
                                           we_head[:, :, piece(n)].bitcast(F32),
                                           ALU.subtract).then_inc(s_wrest, 1)
                f = s - 3
                if f.exists():
                    r = rows[:, f.buf(4)]
                    pool.wait_ge(s_w0, f.times(1, 1))
                    pool.tensor_tensor(r[:, :, W_COL + 1], r[:, :, W_COL], exp_gap[:], ALU.mult).then_inc(s_w1, 1)
                    if f.i is not None or f.c >= 4:
                        pool.wait_ge(s_row[f.buf(4)], (f - 4).uses(4, 64))
                        ids = r[:, :, ID_COL].bitcast(I32)
                        pool.tensor_tensor(ids, ids, id_step[:], ALU.add).then_inc(s_id, 1)
                        pool.wait_ge(s_id, (f - 4).times(1, 1))
                    pool.wait_ge(s_w1, f.times(1, 1))
                    pool.wait_ge(s_pos, f.times(1, 1))
                    settle(pool, s_passed[1])
                    for t in range(NT):
                        for k in range(2):
                            pool.indirect_dma_start(
                                out=bins[k], in_=rows[:, f.buf(4), t, :],
                                out_offset=bass.IndirectOffsetOnAxis(ap=pos[:, f.buf(2), t, k:k + 1], axis=0),
                                in_offset=None).then_inc(s_row[f.buf(4)], 16)

            dense_steps(pool, step, 0, NB + 3)
            for n in range(2):
                pool.wait_ge(s_x1w[n], 16 * (NB // 2))

            def add(k, i):
                for j in range(PAIRS):
                    pool.wait_ge(s_y, i * PAIRS + (k * TRIPS * PAIRS + j + 1))
                    settle(pool, s_passed[1])
                    for t in range(2 * j, 2 * j + 2):
                        pool.indirect_dma_start(
                            out=out, in_=y[:, t, :],
                            out_offset=bass.IndirectOffsetOnAxis(
                                ap=row_in[:, t, ID_COL:ID_COL + 1].bitcast(I32), axis=0),
                            in_offset=None, compute_op=ALU.add).then_inc(s_add[j], 16)

            expert_bodies(pool, add, 0)
            for j in range(PAIRS):
                pool.wait_ge(s_add[j], 32 * TRIPS)
            expert_bodies(pool, add, 1)

        @block.tensor
        def _(pe):
            pe.wait_ge(s_const, 1)
            pe.matmul(ps_rank[:, 0:NT * 2 * E], ones_row[:], bin_base[0:1].rearrange("o t c e -> o (t c e)"),
                      start=True, stop=False, skip_group_check=True).then_inc(s_rank0, 1)

            def project_kv(s):
                pe.wait_ge(s_crest, s.times(1, 1))
                if s.i is not None or s.c >= 1:
                    pe.wait_ge(s_kv, (s - 1).times(1, 1))
                elif s.c == 0:
                    pe.wait_ge(s_wkvr, 1)
                    pe.wait_ge(s_kvb, 16)
                for c in range(KC):
                    head, rest = c_head[:, s.buf(2), c, :], c_rest[:, s.buf(2), c, :]
                    pe.matmul(ps_kv[0:SC, :], head, wkv_head[:, c, :], start=(c == 0), stop=False)
                    pe.matmul(ps_kv[0:SC, :], head, wkv_rest[:, c, :], start=False, stop=False)
                    pe.matmul(ps_kv[0:SC, :], rest, wkv_head[:, c, :], start=False, stop=False)
                pe.matmul(ps_kv[0:SC, :], ones_bf[:, 0:SC], bkv_rows[:], start=False, stop=True).then_inc(s_pkv, 1)

            def attend(b):
                pe.wait_ge(s_q, b.times(2, 2))
                pe.wait_ge(s_m, b.times(1, 1))
                if b.i is not None or b.c >= 1:
                    pe.wait_ge(s_att, (b - 1).times(1, 1))
                for t in range(NT):
                    for c in range(KC):
                        mm = pe.matmul(ps_att[:, t, c * P:(c + 1) * P], q_t[:, c, t, :], kvm[:, c, :],
                                       start=True, stop=True)
                mm.then_inc(s_patt, 1)

            def transpose_h(b):
                pe.wait_ge(s_h, b.times(1, 1))
                if b.i is not None or b.c >= 1:
                    pe.wait_ge(s_ht, (b - 1).times(1, 1))
                for c in range(KC):
                    for t in range(NT):
                        mm = pe.transpose(ps_ht[:, c, t, :], h[:, b.buf(4), t, c * P:(c + 1) * P], ident[:])
                mm.then_inc(s_pht, 1)

            def multiply_ktv(b):
                pe.wait_ge(s_kv, b.times(1, 1))
                if b.i is not None or b.c >= 3:
                    pe.wait_ge(s_sc, (b - 3).times(1, 1))
                for c in range(KC):
                    mm = pe.matmul(ktv[:, c * P:(c + 1) * P], kv[:, 0, c * P:(c + 1) * P],
                                   kv[:, 1, c * P:(c + 1) * P], start=True, stop=True)
                mm.then_inc(s_pm, 1)

            def project_q(b, dc):
                if dc == 0:
                    if b.i is None and b.c == 0:
                        pe.wait_ge(s_w[2], 32)
                    pe.wait_ge(s_ht, b.times(1, 1))
                if b.i is not None or b.c >= 1:
                    pe.wait_ge(s_q, (b - 1).times(2, dc + 1))
                for c in range(KC):
                    mm = pe.matmul(ps_q[dc][:, 0:S], wq[:, c, dc * P:(dc + 1) * P], h_t[:, c, :, :],
                                   start=(c == 0), stop=(c == KC - 1))
                mm.then_inc(s_pq, 1)

            def transpose_h2(b):
                pe.wait_ge(s_h2, b.times(1, 1))
                if b.i is not None or b.c >= 1:
                    pe.wait_ge(s_h2t, (b - 1).times(1, 1))
                for c in range(KC):
                    for t in range(NT):
                        mm = pe.transpose(ps_h2t[:, c, t, :], rows[:, b.buf(4), t, c * P:(c + 1) * P], ident[:])
                mm.then_inc(s_ph2t, 1)

            def gate(b):
                pe.wait_ge(s_h2t, b.times(1, 1))
                pe.wait_ge(s_m, (b + 2).times(1, 1) if (b + 2).exists() else NB)
                if b.i is None and b.c >= NB - 2:
                    pe.wait_ge(s_sc, b.c)
                elif b.i is None and b.c == 0:
                    pe.wait_ge(s_w[3], 48)
                for t in range(NT):
                    for c in range(KC):
                        mm = pe.matmul(logits[:, t, :], h2_t[:, c, t, :], wg[:, c, :],
                                       start=(c == 0), stop=(c == KC - 1))
                mm.then_inc(s_pg, 1)

            def counted(t, weights, b, of):
                return pe.matmul(rank[:, t, :, :], weights[:], onehot[:, b.buf(2), of, :, :],
                                 start=False, stop=False, skip_group_check=True)

            def close_ranks(b):
                pe.wait_ge(s_pick, b.times(1, 1))
                counted(0, not_before, b, 0)
                counted(0, ones_bf, b, 1)
                return counted(1, not_before, b, 1)

            def rank_tokens(b):
                pe.wait_ge(s_oh, b.times(1, 1))
                if b.i is not None or b.c >= 1:
                    close_ranks(b - 1)
                counted(0, before, b, 0)
                counted(1, ones_bf, b, 0)
                counted(1, before, b, 1).then_inc(s_prk, 1)

            def step(s):
                if (s - 1).exists():
                    attend(s - 1)
                if s.exists():
                    transpose_h(s)
                    project_kv(s)
                    project_q(s, 0)
                if (s - 3).exists():
                    rank_tokens(s - 3)
                if (s - 2).exists():
                    transpose_h2(s - 2)
                if s.exists():
                    multiply_ktv(s)
                    project_q(s, 1)
                if (s - 2).exists():
                    gate(s - 2)

            dense_steps(pe, step, 0, NB + 3)
            close_ranks(Batch(None, NB - 1)).then_inc(s_end, 1)

            pe.wait_ge(s_found, 1)
            pe.transpose(ps_kv[0:8, 0:P], found[:].rearrange("p q c h -> p (q c h)"), ident[:]).then_inc(s_tt, 1)

            def transpose_rows(j, loaded):
                pe.wait_ge(s_in[j], loaded)
                for t in range(2):
                    for c in range(KC):
                        mm = pe.transpose(ps_rt[j % 2][:, t, c, :], row_in[:, 2 * j + t, c * P:(c + 1) * P],
                                          ident[:])
                mm.then_inc(s_prt, 1)

            pe.wait_ge(s_table, 1)
            offsets = table_reader(nc, pe, table, 1, (E - 1) * D)

            def multiply(k, i):
                at = offsets(k, i)
                for j in range(PAIRS):
                    last = isinstance(i, int) and k == 1 and i == TRIPS - 1 and j == PAIRS - 1
                    if not last:
                        transpose_rows((j + 1) % PAIRS, i * 32 + 32 * (k * TRIPS + 1 + (j + 1) // PAIRS))
                    number = i * PAIRS + (k * TRIPS * PAIRS + j)
                    pe.wait_ge(s_rt, number + 1)
                    for t in range(2):
                        o = ps_y[j % YB][:, t, :]
                        for c in range(KC):
                            heads, rests = row_head[:, j % 2, t, c, :], row_rest[:, j % 2, t, c, :]
                            w_head = we_head[:, c, bass.ds(at[2 * j + t], D)]
                            pe.matmul(o, heads, w_head, start=(c == 0), stop=False)
                            pe.matmul(o, rests, w_head, start=False, stop=False)
                            pe.matmul(o, heads, we_rest[:, c, bass.ds(at[2 * j + t], D)], start=False, stop=False)
                        mm = pe.matmul(o, ones_bf[:], be_rows[:, bass.ds(at[2 * j + t], D)],
                                       start=False, stop=True)
                    mm.then_inc(s_py, 1)

            pe.wait_ge(s_wrest, WE_PIECES)
            pe.wait_ge(s_eb, 16)
            transpose_rows(0, 32)
            expert_bodies(pe, multiply, 0, peel_last=True)
            expert_bodies(pe, multiply, 1, peel_last=True)

        @block.scalar
        def _(act):
            act.add_instruction(mybir.InstLoadActFuncSet(name=nc.get_next_instruction_name(),
                                                         act_func_set_id=LOG_EXP_SET, ins=[], outs=[]))
            act.wait_ge(s_zero, 1)

            def context_head(b):
                act.wait_ge(s_c[b.buf(4)], b.uses(4, 16))
                if b.i is not None or b.c >= 2:
                    act.wait_ge(s_pkv, (b - 2).times(1, 1))
                act.activation(c_head[:, b.buf(2)], c_sb[:, b.buf(4)], ACT.Copy).then_inc(s_chead, 1)

            context_head(Batch(None, 0))
            act.wait_ge(s_w[0], 16)
            act.activation(wkv_head[:], wkv, ACT.Copy).then_inc(s_wkvh, 1)

            def inverse_root(n, b):
                act.wait_ge(s_mv[n], b.times(1, 1))
                act.activation(lnv[:, n, :], mv[:, n, b.buf(2), :, 1], ACT.Ln, bias=eps[:, 0:1]).then_inc(s_ln[n], 1)
                act.wait_ge(s_ln[n], b.times(1, 1))
                act.activation(rstd[:, n, b.buf(2), :], lnv[:, n, :], ACT.Exp, scale=-0.5).then_inc(s_rstd[n], 1)

            def copy_q(b, dc):
                act.wait_ge(s_pq, b.times(2, dc + 1))
                if dc == 0 and (b.i is not None or b.c >= 1):
                    act.wait_ge(s_patt, (b - 1).times(1, 1))
                if b.i is None and b.c == 0:
                    act.wait_ge(s_w[2], 32)
                act.activation(q_t[:, dc, :, :].rearrange("p t n -> p (t n)"), ps_q[dc][:, 0:S], ACT.Identity,
                               bias=bq_sb[:, dc:dc + 1]).then_inc(s_q, 1)

            def gate_exps(b):
                act.wait_ge(s_gap, b.times(1, 1))
                if b.i is not None or b.c >= 1:
                    act.wait_ge(s_w1, (b - 1).times(1, 1))
                for t in range(NT):
                    act.activation(exps[:, t, :], scores[:, t, :], ACT.Exp, bias=neg_max[:, t:t + 1],
                                   accum_out=sums[:, t:t + 1])
                act.activation(exp_gap[:], gap[:], ACT.Exp).then_inc(s_exp, 1)

            def normalise_h2(b):
                act.wait_ge(s_nmr[2], b.times(1, 1))
                if b.i is not None or b.c >= 4:
                    act.wait_ge(s_row[b.buf(4)], (b - 4).uses(4, 64))
                for t in range(NT):
                    a = act.activation(rows[:, b.buf(4), t, 0:D], x1[:, b.buf(2), t, :], ACT.Identity,
                                       bias=nmr[:, 2, t:t + 1], scale=rstd[:, 2, b.buf(2), t:t + 1])
                a.then_inc(s_h2, 1)

            def copy_kv(b):
                act.wait_ge(s_pkv, b.times(1, 1))
                if b.i is not None or b.c >= 1:
                    act.wait_ge(s_pm, (b - 1).times(1, 1))
                act.activation(kv[:].rearrange("p a d -> p (a d)"), ps_kv[0:SC, :], ACT.Copy).then_inc(s_kv, 1)

            def normalise_x(b):
                act.wait_ge(s_nmr[0], b.times(1, 1))
                if b.i is not None or b.c >= 4:
                    act.wait_ge(s_att, (b - 4).times(1, 1))
                    act.wait_ge(s_pht, (b - 4).times(1, 1))
                for t in range(NT):
                    a = act.activation(h[:, b.buf(4), t, :], x_sb[:, b.buf(4), t, :], ACT.Identity,
                                       bias=nmr[:, 0, t:t + 1], scale=rstd[:, 0, b.buf(2), t:t + 1])
                a.then_inc(s_h, 1)

            def copy_h_t(b):
                act.wait_ge(s_pht, b.times(1, 1))
                if b.i is not None or b.c >= 1:
                    act.wait_ge(s_pq, (b - 1).times(2, 2))
                act.activation(h_t[:], ps_ht[:], ACT.Copy).then_inc(s_ht, 1)

            def copy_h2_t(b):
                act.wait_ge(s_ph2t, b.times(1, 1))
                if b.i is not None or b.c >= 1:
                    act.wait_ge(s_pg, (b - 1).times(1, 1))
                act.activation(h2_t[:], ps_h2t[:], ACT.Copy).then_inc(s_h2t, 1)

            def step(s):
                p, b, f, nxt = s - 1, s - 2, s - 3, s + 1
                if b.exists():
                    inverse_root(2, b)
                if s.exists():
                    copy_h_t(s)
                if b.exists():
                    normalise_h2(b)
                if nxt.exists():
                    inverse_root(0, nxt)
                if s.exists():
                    copy_kv(s)
                if f.exists():
                    gate_exps(f)
                if p.exists():
                    inverse_root(1, p)
                if b.exists():
                    copy_h2_t(b)
                if s.exists():
                    copy_q(s, 0)
                    copy_q(s, 1)
                if nxt.exists():
                    normalise_x(nxt)
                if (s + 2).exists():
                    context_head(s + 2)
                for n in pieces(s.c, 2) if s.i is None and s.c >= 0 else ():
                    act.wait_ge(s_we[n], 16)
                    act.activation(we_head[:, :, piece(n)], we[:, :, piece(n)], ACT.Copy).then_inc(s_whead, 1)

            dense_steps(act, step, -1, NB + 3)

            fill(act, 0, E // 2, E)

            def weigh(k, i):
                for j in range(PAIRS):
                    act.wait_ge(s_py, i * PAIRS + (k * TRIPS * PAIRS + j + 1))
                    if not (isinstance(i, int) and k == 0):
                        act.wait_ge(s_add[j], i * 32 + 32 * k * TRIPS)
                    for t in range(2):
                        a = act.activation(y[:, 2 * j + t, :], ps_y[j % YB][:, t, :], ACT.Relu,
                                           scale=row_in[:, 2 * j + t, W_COL + k:W_COL + k + 1])
                    a.then_inc(s_y, 1)

            for k in range(2):
                expert_bodies(act, weigh, k, peel_first=(k == 0))

        @block.vector
        def _(dve):
            dve.memset(eps[:], EPS).then_inc(s_zero, 1)
            dve.memset(bkv_rows[:].bitcast(U32), 0).then_inc(s_zero, 1)

            def split(src, rest, part, n):
                dve.tensor_copy(part[:, 0, :], src).then_inc(s_split, 1)
                dve.wait_ge(s_split, n + 1)
                dve.tensor_tensor(rest[:, 0, :], src, part[:, 0, :], ALU.subtract).then_inc(s_split, 1)
                dve.wait_ge(s_split, n + 2)
                dve.tensor_copy(part[:, 1, :], rest[:, 0, :]).then_inc(s_split, 1)
                dve.wait_ge(s_split, n + 3)
                dve.tensor_tensor(rest[:, 1, :], rest[:, 0, :], part[:, 1, :], ALU.subtract).then_inc(s_split, 1)
                dve.wait_ge(s_split, n + 4)
                dve.tensor_copy(part[:, 2, :], rest[:, 1, :]).then_inc(s_split, 1)

            def stats(n, b, src):
                for t in range(NT):
                    i = dve.bn_stats(st[:, n, t, :], src[:, t, :])
                i.then_inc(s_st[n], 1)

            def moments(n, b):
                for t in range(NT):
                    i = dve.bn_aggr(mv[:, n, b.buf(2), t, :], st[:, n, t, :])
                i.then_inc(s_mv[n], 1)

            def mean_shift(n, b):
                dve.wait_ge(s_rstd[n], b.times(1, 1))
                dve.scalar_tensor_tensor(out=nmr[:, n, :], in0=mv[:, n, b.buf(2), :, 0], scalar=-1.0,
                                         in1=rstd[:, n, b.buf(2), :], op0=ALU.mult,
                                         op1=ALU.mult).then_inc(s_nmr[n], 1)

            def place(b):
                dve.wait_ge(s_sum, b.times(1, 1))
                if b.i is not None or b.c >= 2:
                    dve.wait_ge(s_row[(b - 2).buf(4)], (b - 2).uses(4, 64))
                dve.scalar_tensor_tensor(out=pos[:, b.buf(2)].rearrange("p t c -> p (t c)"),
                                         in0=signed_pos[:], scalar=-1.0, in1=signed_pos[:],
                                         op0=ALU.mult, op1=ALU.max).then_inc(s_pos, 1)

            def copy_scores(b):
                dve.wait_ge(s_pg, b.times(1, 1))
                if b.i is not None or b.c >= 1:
                    dve.wait_ge(s_exp, (b - 1).times(1, 1))
                dve.tensor_copy(scores[:], logits).then_inc(s_sc, 1)

            def top_values(b):
                for t in range(NT):
                    i = dve.max(top[:, t, :], scores[:, t, :])
                i.then_inc(s_top, 1)

            def score_gaps(b):
                dve.wait_ge(s_top, b.times(1, 1))
                dve.tensor_scalar(neg_max[:], top[:, :, 0], -1.0, None, ALU.mult)
                dve.tensor_tensor(gap[:], top[:, :, 1], top[:, :, 0], ALU.subtract).then_inc(s_gap, 1)

            def top_indices(b):
                for t in range(NT):
                    i = dve.max_index(top_i[:, t, :], top[:, t, :], scores[:, t, :])
                i.then_inc(s_topi, 1)

            def indices_as_floats(b):
                dve.wait_ge(s_topi, b.times(1, 1))
                dve.tensor_copy(top_f[:], top_i[:, :, 0:2]).then_inc(s_topf, 1)

            def mark_experts(b):
                dve.wait_ge(s_topf, b.times(1, 1))
                dve.tensor_tensor(onehot[:, b.buf(2)].rearrange("p t c e -> p (t c) e"),
                                  iota_e[:].unsqueeze(1).to_broadcast([P, NT * 2, E]),
                                  top_f[:].rearrange("p t c -> p (t c)").unsqueeze(2)
                                  .to_broadcast([P, NT * 2, E]), ALU.is_equal).then_inc(s_oh, 1)

            def first_weights(b):
                dve.wait_ge(s_exp, b.times(1, 1))
                dve.reciprocal(rows[:, b.buf(4), :, W_COL], sums[:]).then_inc(s_w0, 1)

            def pick_ranks(b):
                dve.wait_ge(s_prk, b.times(1, 1))
                dve.tensor_tensor(picked[:], rank.rearrange("p t c e -> p (t c) e"),
                                  onehot[:, b.buf(2)].rearrange("p t c e -> p (t c) e"),
                                  ALU.mult).then_inc(s_pick, 1)

            def sum_ranks(b):
                dve.wait_ge(s_pick, b.times(1, 1))
                dve.tensor_reduce(signed_pos[:], picked[:], AX_X, ALU.add).then_inc(s_sum, 1)

            def add_attention(b):
                dve.wait_ge(s_patt, b.times(1, 1))
                dve.wait_ge(s_h, b.times(1, 1))
                dve.tensor_tensor(att[:], ps_att[:], h[:, b.buf(4)], ALU.add).then_inc(s_att, 1)

            def mask_ktv(b):
                dve.wait_ge(s_pm, b.times(1, 1))
                if b.i is not None or b.c >= 1:
                    dve.wait_ge(s_patt, (b - 1).times(1, 1))
                dve.tensor_tensor(kvm[:].rearrange("p c n -> p (c n)"), ktv,
                                  head_mask[:].rearrange("p c n -> p (c n)"), ALU.mult).then_inc(s_m, 1)

            def scale(b):
                dve.wait_ge(s_mv[1], b.times(1, 1))
                for t in range(NT):
                    i = dve.scalar_tensor_tensor(out=scaled[:, t, :], in0=att[:, t, :],
                                                 scalar=mv[:, 1, b.buf(2), t, 0:1], in1=gamma_sb[:],
                                                 op0=ALU.subtract, op1=ALU.mult)
                i.then_inc(s_scaled, 1)

            def finish_x1(b):
                dve.wait_ge(s_scaled, b.times(1, 1))
                dve.wait_ge(s_rstd[1], b.times(1, 1))
                dve.wait_ge(s_xb, b.times(1, 1))
                if b.i is not None or b.c >= 2:
                    dve.wait_ge(s_h2, (b - 2).times(1, 1))
                    dve.wait_ge(s_x1w[b.buf(2)], (b - 2).uses(2, 16))
                for t in range(NT):
                    dve.scalar_tensor_tensor(out=x1[:, b.buf(2), t, :], in0=scaled[:, t, :],
                                             scalar=rstd[:, 1, b.buf(2), t:t + 1],
                                             in1=x_beta[:, b.buf(2), t, :], op0=ALU.mult,
                                             op1=ALU.add).then_inc(s_x1, 1)

            def step(s):
                p, b, f, g, nxt = s - 1, s - 2, s - 3, s - 4, s + 1
                if s.i is None and s.c == 0:
                    dve.memset(zeros, 0.0).then_inc(s_zero, 1)
                    dve.wait_ge(s_wkvh, 1)
                    dve.tensor_tensor(wkv_rest[:], wkv, wkv_head[:].bitcast(F32), ALU.subtract).then_inc(s_wkvr, 1)
                    dve.wait_ge(s_const, 1)
                if s.i is None and s.c == 1:
                    dve.memset(be_rows[:].bitcast(U32), 0).then_inc(s_zero, 1)
                    dve.wait_ge(s_be_in, 16)
                    split(be_in[:], be_rest, be_part, 5)
                    dve.wait_ge(s_w[3], 48)
                if b.exists():
                    for t in range(NT):
                        dve.wait_ge(s_x1, b.times(NT, t + 1))
                        i = dve.bn_stats(st[:, 2, t, :], x1[:, b.buf(2), t, :])
                    i.then_inc(s_st[2], 1)
                if g.exists():
                    place(g)
                if f.exists():
                    copy_scores(f)
                if b.exists():
                    dve.wait_ge(s_st[2], b.times(1, 1))
                    settle(dve, s_passed[0])
                    moments(2, b)
                if f.exists():
                    dve.wait_ge(s_sc, f.times(1, 1))
                    settle(dve, s_passed[0])
                    top_values(f)
                if nxt.exists():
                    dve.wait_ge(s_x[nxt.buf(4)], nxt.uses(4, 16))
                    if nxt.i is not None or nxt.c >= 1:
                        dve.wait_ge(s_mv[0], (nxt - 1).times(1, 1))
                    stats(0, nxt, x_sb[:, nxt.buf(4)])
                if b.exists():
                    mean_shift(2, b)
                if f.exists():
                    score_gaps(f)
                if nxt.exists():
                    dve.wait_ge(s_st[0], nxt.times(1, 1))
                if nxt.exists() or f.exists():
                    settle(dve, s_passed[0])
                if f.exists():
                    top_indices(f)
                if nxt.exists():
                    moments(0, nxt)
                if f.exists():
                    indices_as_floats(f)
                if p.exists():
                    add_attention(p)
                if f.exists():
                    mark_experts(f)
                if p.exists():
                    dve.wait_ge(s_att, p.times(1, 1))
                    stats(1, p, att)
                if nxt.exists():
                    mean_shift(0, nxt)
                if p.exists():
                    dve.wait_ge(s_st[1], p.times(1, 1))
                    settle(dve, s_passed[0])
                    moments(1, p)
                if f.exists():
                    pick_ranks(f)
                if p.exists():
                    scale(p)
                if s.exists():
                    mask_ktv(s)
                if f.exists():
                    first_weights(f)
                    sum_ranks(f)
                if p.exists():
                    finish_x1(p)

            dve.wait_ge(s_w[1], 16)
            split(bkv_in[:], bkv_rest, bkv_part, 0)
            dense_steps(dve, step, -1, NB + 4)

            steps = [0]

            def done(*ins):
                steps[0] += 1
                ins[-1].then_inc(s_tab, 1)
                dve.wait_ge(s_tab, steps[0])

            base0 = bin_base[:, 0]
            dve.wait_ge(s_end, 1)
            done(dve.tensor_copy(ends[:], rank[:, 0]))
            pairs = ends[:].rearrange("p c (r o) -> p c r o", o=2)
            pad_pairs = pad_at[:].rearrange("p c (r o) -> p c r o", o=2)
            dve.tensor_copy(pad_pairs[:, :, :, 0], pairs[:, :, :, 0])
            dve.tensor_scalar(pad_pairs[:, :, :, 1], pairs[:, :, :, 1], -1.0, float(1 - P), ALU.mult,
                              ALU.add).then_inc(s_pad, 1)
            done(dve.tensor_tensor(counts[:], ends[:], base0, ALU.subtract))
            done(dve.tensor_scalar(cnt_i[:], counts[:], float(P - 1), None, ALU.add))
            done(dve.tensor_scalar(tiles_i[:], cnt_i[:], P.bit_length() - 1, None, ALU.logical_shift_right))
            done(dve.tensor_copy(tiles_f[:], tiles_i[:]), dve.tensor_copy(scan[:, 0], tiles_i[:]))
            sh = shift[:, :, 0:E].rearrange("p c (r o) -> p c r o", o=2)
            bp = base0.rearrange("p c (r o) -> p c r o", o=2)
            tp = tiles_f[:].rearrange("p c (r o) -> p c r o", o=2)
            dve.tensor_copy(sh[:, :, :, 0], bp[:, :, :, 0])
            for k in range(2):
                dve.scalar_tensor_tensor(out=sh[:, k, :, 1], in0=tp[:, k, :, 1], scalar=float(P),
                                         in1=bp[:, k, :, 1], op0=ALU.mult, op1=ALU.add)
            a, d = 0, 1
            while d < E:
                done(dve.tensor_copy(scan[:, 1 - a, :, 0:d], scan[:, a, :, 0:d]),
                     dve.tensor_tensor(scan[:, 1 - a, :, d:E], scan[:, a, :, d:E], scan[:, a, :, 0:E - d],
                                       ALU.add))
                a, d = 1 - a, 2 * d
            upto, before_e = scan[:, a], scan[:, 1 - a]
            done(dve.tensor_scalar(sh[:, :, :, 1], sh[:, :, :, 1], -1.0, 1.0, ALU.mult, ALU.add),
                 dve.tensor_scalar(shift[:, :, E], upto[:, :, E - 1], -float(P), float(SPARE), ALU.mult, ALU.add),
                 dve.tensor_tensor(before_e, upto, tiles_f[:], ALU.subtract))
            done(dve.scalar_tensor_tensor(out=shift[:, :, 0:E], in0=before_e, scalar=-float(P),
                                          in1=shift[:, :, 0:E], op0=ALU.mult, op1=ALU.add),
                 dve.tensor_tensor(reached[:], tile_no[:].unsqueeze(1).unsqueeze(3).to_broadcast([P, 2, 2, E]),
                                   upto.unsqueeze(2).to_broadcast([P, 2, 2, E]), ALU.is_ge))
            done(dve.tensor_tensor(delta[:], shift[:, :, 1:E + 1], shift[:, :, 0:E], ALU.subtract),
                 dve.tensor_reduce(found[:, 1], reached[:], AX_X, ALU.add))
            done(dve.tensor_tensor(reached_d[:], reached[:],
                                   delta[:].unsqueeze(2).to_broadcast([P, 2, 2, E]), ALU.mult))
            done(dve.tensor_reduce(found[:, 0], reached_d[:], AX_X, ALU.add))
            done(dve.tensor_tensor(found[:, 0], found[:, 0],
                                   shift[:, :, 0:1].to_broadcast([P, 2, 2]), ALU.add))
            dve.scalar_tensor_tensor(out=found[:, 0], in0=tile_no[:].unsqueeze(1).to_broadcast([P, 2, 2]),
                                     scalar=float(P), in1=found[:, 0], op0=ALU.mult, op1=ALU.add)
            dve.tensor_scalar(found[:, 1], found[:, 1], float(E - 1), float(D), ALU.min,
                              ALU.mult).then_inc(s_found, 1)
            dve.wait_ge(s_tt, 1)
            dve.tensor_copy(table[:], ps_kv[0:8, 0:P]).then_inc(s_table, 1)

            def copy_rows(k, i):
                for j in range(PAIRS):
                    number = i * PAIRS + (k * TRIPS * PAIRS + j)
                    dve.wait_ge(s_prt, number + 1)
                    if not (isinstance(i, int) and k == 0 and j < 2):
                        dve.wait_ge(s_py, number - 1)
                    if not (isinstance(i, int) and k == 0 and j < YB):
                        dve.wait_ge(s_y, number + 1 - YB)
                    dve.tensor_copy(row_head[:, j % 2], ps_rt[j % 2][:]).then_inc(s_rhead, 1)
                    dve.wait_ge(s_rhead, number + 1)
                    dve.tensor_tensor(row_rest[:, j % 2], ps_rt[j % 2][:], row_head[:, j % 2].bitcast(F32),
                                      ALU.subtract).then_inc(s_rt, 1)

            for k in range(2):
                expert_bodies(dve, copy_rows, k, peel_first=(k == 0))


def kernel(**inputs):
    import numpy as np
    import concourse.bacc as bacc
    from concourse.bass_utils import run_bass_kernel_spmd

    g = {n.replace("L0_xattn_", "").replace("L0_ffn_", ""): np.asarray(v) for n, v in inputs.items()}
    c = np.ascontiguousarray
    arrays = {
        "x": c(g["x"].reshape(TOK, D)),
        "ctx_t": c(g["ctx_1024"].transpose(0, 2, 1).reshape(NB, KC, P, SC).transpose(0, 2, 1, 3)),
        "wkv_t": c(np.concatenate([g["Wk"].T, g["Wv"].T], axis=1)),
        "wq_t": c(g["Wq"].T),
        "gate_t": c(g["gate_w"].T),
        "we_t": c(g["expert_w"].transpose(2, 0, 1).reshape(D, E * D)),
        "bkv": c(np.concatenate([g["bk"], g["bv"]])),
        "be": c(g["expert_b"].reshape(E * D)),
        "bq": c(g["bq"].reshape(KC, P).T),
        "gamma": c(g["ln_gamma"]),
        "beta": c(g["ln_beta"]),
    }
    nc = bacc.Bacc("TRN2", target_bir_lowering=False, num_devices=1)
    args = [nc.dram_tensor(f"in_{n}", a.shape, mybir.dt.from_np(a.dtype), kind="ExternalInput").ap()
            for n, a in arrays.items()]
    out = nc.dram_tensor("out_rows", (OUT_ROWS, D), F32, kind="ExternalOutput").ap()
    build(nc, *args, out)
    r = run_bass_kernel_spmd(nc, [{f"in_{n}": a for n, a in arrays.items()}], core_ids=[0])
    return r.results[0]["out_rows"][0:TOK].reshape(NB, S, D)
```
